# Optimizing a Trainium2 kernel written in Bass

```python
import numpy as np
import jax
import jax.numpy as jnp

def _softmax(x, axis=-1):
    return jax.nn.softmax(x, axis=axis)

def _gelu(x):
    return jax.nn.gelu(x, approximate=True)

def _silu(x):
    return jax.nn.silu(x)

def _sigmoid(x):
    return jax.nn.sigmoid(x)

def _layernorm(x, axis=-1, eps=1e-05):
    m = jnp.mean(x, axis=axis, keepdims=True)
    v = jnp.var(x, axis=axis, keepdims=True)
    return (x - m) / jnp.sqrt(v + eps)

def _scatter_add(tgt, idx, src, axis=0):
    return tgt.at[idx].add(src)

def _segment_sum(src, seg, n):
    return jax.ops.segment_sum(src, seg, n)
kernel_name = 'mk_xattn_ffn_d1_seqx_r8_136057'

def setup_inputs(seed: int=0):
    np.random.seed(seed)
    _w = jnp.asarray

    def _rec_inputs():
        import jax
        import jax.numpy as jnp
        _rk = jax.random.key(seed)
        x = 7.22e-05 + 1 * jax.random.normal(jax.random.fold_in(_rk, 1), (16, 128, 256), jnp.float32)
        _lenS = 128 - jax.random.randint(jax.random.fold_in(_rk, 7), (16,), 0, max(1, 128 // 4) + 1, jnp.int32)
        _lenS2 = 128 - jax.random.randint(jax.random.fold_in(_rk, 8), (16,), 0, max(1, 128 // 4) + 1, jnp.int32)
        _ctx_1024P = jax.random.normal(jax.random.fold_in(_rk, 11), (16, 16, 128), jnp.float32)
        _ctx_1024c = jax.random.dirichlet(jax.random.fold_in(_rk, 511), 0.3 * jnp.ones((16,), jnp.float32), (16, 128))
        _ctx_1024t = jnp.einsum('bsk,bkd->bsd', _ctx_1024c, _ctx_1024P)
        _ctx_1024t = _ctx_1024t * jax.lax.rsqrt(jnp.mean(jnp.square(_ctx_1024t)) + 1e-12) * 0.953939
        ctx_1024 = -1.39393e-06 + 0.999914 * (_ctx_1024t + 0.3 * jax.random.normal(jax.random.fold_in(_rk, 611), (16, 128, 128), jnp.float32))
        fside_BxSx2_0 = jax.random.uniform(jax.random.fold_in(_rk, 12), (16, 128, 2), jnp.float32, 0.0, 0.999707)
        return (x, ctx_1024, fside_BxSx2_0)
    x, ctx_1024, fside_BxSx2_0 = _rec_inputs()

    def _L0_xattn_setup():
        import jax, jax.numpy as jnp
        import numpy as np
        DIM = 256
        CTX_DIM = 128
        N_HEADS = 32
        HEAD_DIM = DIM // N_HEADS
        POS_DIM = 2
        B, N, CTXN = (2, 256, 256)
        ROPE_BASE = 10000.0

        def apply_axial_rope(x, pos):
            b, n, h, d = x.shape
            p = pos.shape[-1]
            dpa = d // p
            half = dpa // 2
            freqs = ROPE_BASE ** (-jnp.arange(half, dtype=x.dtype) / half)
            ang = pos[..., :, None] * freqs
            cos = jnp.cos(ang)[:, :, None, :, :]
            sin = jnp.sin(ang)[:, :, None, :, :]
            xr = x.reshape(b, n, h, p, half, 2)
            x1, x2 = (xr[..., 0], xr[..., 1])
            out = jnp.stack([x1 * cos - x2 * sin, x1 * sin + x2 * cos], axis=-1)
            return out.reshape(b, n, h, d)
        key = jax.random.key(seed)
        ks = jax.random.split(key, 8)
        x = jax.random.normal(ks[0], (B, N, DIM), jnp.float32)
        ctx = jax.random.normal(ks[1], (B, CTXN, CTX_DIM), jnp.float32)
        pos_map = jax.random.uniform(ks[2], (B, N, POS_DIM), jnp.float32)
        ctx_pos_map = jax.random.uniform(ks[3], (B, CTXN, POS_DIM), jnp.float32)
        Wq = jax.random.normal(ks[4], (DIM, DIM), jnp.float32) / np.sqrt(DIM)
        Wkv = jax.random.normal(ks[5], (CTX_DIM, 2 * DIM), jnp.float32) / np.sqrt(CTX_DIM)
        Wout = jax.random.normal(ks[6], (DIM, DIM), jnp.float32) / np.sqrt(DIM)
        bout = jnp.zeros((DIM,), jnp.float32)
        return {'x': x, 'ctx': ctx, 'pos_map': pos_map, 'ctx_pos_map': ctx_pos_map, 'Wq': Wq, 'Wkv': Wkv, 'Wout': Wout, 'bout': bout}
    _L0_xattn_all = _L0_xattn_setup()
    _L0_xattn_in = {k: v for k, v in _L0_xattn_all.items() if k in ('Wq', 'Wkv', 'Wout', 'bout')}
    del _L0_xattn_all

    def _L0_ffn_setup():
        import jax, jax.numpy as jnp
        import numpy as np
        BITS = 4
        SIGNED_MIN, SIGNED_MAX = (-2 ** (BITS - 1), 2 ** (BITS - 1) - 1)
        UNSIGNED_MIN, UNSIGNED_MAX = (0, 2 ** BITS - 1)
        INT32_MIN, INT32_MAX = (-2.0 ** 31, 2.0 ** 31 - 1)

        def fake_quant(x, scale, qmin, qmax):
            q = jnp.clip(jnp.round(x / scale), qmin, qmax) * scale
            return x + jax.lax.stop_gradient(q - x)

        def weight_scale(W):
            return jax.lax.stop_gradient(jnp.max(jnp.abs(W))) / SIGNED_MAX
        key = jax.random.key(seed)
        ks = jax.random.split(key, 5)
        B, S, D, F = (4, 256, 256, 1024)
        return {'x': jax.random.normal(ks[0], (B, S, D), dtype=jnp.float32), 'W1': jax.random.normal(ks[1], (F, D), dtype=jnp.float32) * 0.02, 'b1': jax.random.normal(ks[2], (F,), dtype=jnp.float32) * 0.02, 'W2': jax.random.normal(ks[3], (D, F), dtype=jnp.float32) * 0.02, 'b2': jax.random.normal(ks[4], (D,), dtype=jnp.float32) * 0.02, 's_act1': jnp.full((1,), 0.1, dtype=jnp.float32), 's_act2': jnp.full((1,), 0.1, dtype=jnp.float32)}
    _L0_ffn_all = _L0_ffn_setup()
    _L0_ffn_in = {k: v for k, v in _L0_ffn_all.items() if k in ('W1', 'b1', 'W2', 'b2', 's_act1', 's_act2')}
    del _L0_ffn_all
    return {'x': x, 'ctx_1024': ctx_1024, 'fside_BxSx2_0': fside_BxSx2_0, 'L0_xattn_Wq': _L0_xattn_in['Wq'], 'L0_xattn_Wkv': _L0_xattn_in['Wkv'], 'L0_xattn_Wout': _L0_xattn_in['Wout'], 'L0_xattn_bout': _L0_xattn_in['bout'], 'L0_ffn_W1': _L0_ffn_in['W1'], 'L0_ffn_b1': _L0_ffn_in['b1'], 'L0_ffn_W2': _L0_ffn_in['W2'], 'L0_ffn_b2': _L0_ffn_in['b2'], 'L0_ffn_s_act1': _L0_ffn_in['s_act1'], 'L0_ffn_s_act2': _L0_ffn_in['s_act2']}

def reference(x, ctx_1024, fside_BxSx2_0, L0_xattn_Wq, L0_xattn_Wkv, L0_xattn_Wout, L0_xattn_bout, L0_ffn_W1, L0_ffn_b1, L0_ffn_W2, L0_ffn_b2, L0_ffn_s_act1, L0_ffn_s_act2):
    import jax
    import jax.numpy as jnp

    def _L0_xattn_ref(x, ctx, pos_map, ctx_pos_map, Wq, Wkv, Wout, bout):
        import jax, jax.numpy as jnp
        import numpy as np
        DIM = 256
        CTX_DIM = 128
        N_HEADS = 32
        HEAD_DIM = DIM // N_HEADS
        POS_DIM = 2
        B, N, CTXN = (2, 256, 256)
        ROPE_BASE = 10000.0

        def apply_axial_rope(x, pos):
            b, n, h, d = x.shape
            p = pos.shape[-1]
            dpa = d // p
            half = dpa // 2
            freqs = ROPE_BASE ** (-jnp.arange(half, dtype=x.dtype) / half)
            ang = pos[..., :, None] * freqs
            cos = jnp.cos(ang)[:, :, None, :, :]
            sin = jnp.sin(ang)[:, :, None, :, :]
            xr = x.reshape(b, n, h, p, half, 2)
            x1, x2 = (xr[..., 0], xr[..., 1])
            out = jnp.stack([x1 * cos - x2 * sin, x1 * sin + x2 * cos], axis=-1)
            return out.reshape(b, n, h, d)
        b, n, _ = x.shape
        ctx_n = ctx.shape[1]
        q = (x @ Wq).reshape(b, n, N_HEADS, HEAD_DIM)
        k, v = jnp.split(ctx @ Wkv, 2, axis=-1)
        k = k.reshape(b, ctx_n, N_HEADS, HEAD_DIM)
        v = v.reshape(b, ctx_n, N_HEADS, HEAD_DIM)
        q = apply_axial_rope(q, pos_map)
        k = apply_axial_rope(k, ctx_pos_map)
        scale = 1.0 / np.sqrt(HEAD_DIM).astype(np.float32)
        logits = jnp.einsum('bqhd,bkhd->bhqk', q, k) * scale
        w = jax.nn.softmax(logits, axis=-1)
        attn = jnp.einsum('bhqk,bkhd->bqhd', w, v)
        attn = attn.reshape(b, n, N_HEADS * HEAD_DIM)
        return attn @ Wout + bout

    def _L0_ffn_ref(x, W1, b1, W2, b2, s_act1, s_act2):
        import jax, jax.numpy as jnp
        import numpy as np
        BITS = 4
        SIGNED_MIN, SIGNED_MAX = (-2 ** (BITS - 1), 2 ** (BITS - 1) - 1)
        UNSIGNED_MIN, UNSIGNED_MAX = (0, 2 ** BITS - 1)
        INT32_MIN, INT32_MAX = (-2.0 ** 31, 2.0 ** 31 - 1)

        def fake_quant(x, scale, qmin, qmax):
            q = jnp.clip(jnp.round(x / scale), qmin, qmax) * scale
            return x + jax.lax.stop_gradient(q - x)

        def weight_scale(W):
            return jax.lax.stop_gradient(jnp.max(jnp.abs(W))) / SIGNED_MAX
        s1 = s_act1[0]
        s2 = s_act2[0]
        x_q = fake_quant(x, s1, SIGNED_MIN, SIGNED_MAX)
        sw1 = weight_scale(W1)
        W1_q = fake_quant(W1, sw1, SIGNED_MIN, SIGNED_MAX)
        b1_q = fake_quant(b1, s1 * sw1, INT32_MIN, INT32_MAX)
        h = jnp.einsum('bsd,fd->bsf', x_q, W1_q) + b1_q
        h_q = fake_quant(jax.nn.relu(h), s2, UNSIGNED_MIN, UNSIGNED_MAX)
        sw2 = weight_scale(W2)
        W2_q = fake_quant(W2, sw2, SIGNED_MIN, SIGNED_MAX)
        b2_q = fake_quant(b2, s2 * sw2, INT32_MIN, INT32_MAX)
        out = jnp.einsum('bsf,df->bsd', h_q, W2_q) + b2_q
        return out
    x = x + _L0_xattn_ref(_layernorm(x, axis=-1), ctx_1024, fside_BxSx2_0, fside_BxSx2_0, L0_xattn_Wq, L0_xattn_Wkv, L0_xattn_Wout, L0_xattn_bout)
    x = x + _L0_ffn_ref(_layernorm(x, axis=-1), L0_ffn_W1, L0_ffn_b1, L0_ffn_W2, L0_ffn_b2, L0_ffn_s_act1, L0_ffn_s_act2)
    return x

_drawn_inputs = setup_inputs


def setup_inputs(seed=0):
    import zlib

    import numpy as np

    out = dict(_drawn_inputs(seed))
    spreads = {'L0_xattn_bout': (0.0, 0.1)}
    factors = {'L0_ffn_b1': 4.184, 'L0_ffn_b2': 3.343}
    for name, (base, spread) in spreads.items():
        noise = np.random.default_rng([zlib.crc32(name.encode()), seed]).standard_normal(out[name].shape)
        drawn = base * np.exp(spread * noise) if base else spread * noise
        out[name] = jnp.asarray(drawn.astype(out[name].dtype))
    for name, factor in factors.items():
        out[name] = (out[name] * factor).astype(out[name].dtype)
    return out
```

```python
import numpy as np
import concourse.bass as bass
from concourse import mybir
from contextlib import ExitStack

F32 = mybir.dt.float32
F32R = mybir.dt.float32r
BF16 = mybir.dt.bfloat16
I16 = mybir.dt.int16
I32 = mybir.dt.int32
ALU = mybir.AluOpType
ACT = mybir.ActivationFunctionType
AX = mybir.AxisListType

BATCH, TOK, DIM, CTX, HEADS, FFN = 16, 128, 256, 128, 32, 1024
HD = DIM // HEADS
GROUPS = HEADS // 4
DC = DIM // 128
FC = FFN // 128
EPS = 1e-5
SCALE = 1.0 / float(np.sqrt(np.float32(HD)))
QMIN, QMAX, HMAX = -8.0, 7.0, 15.0
ROPE_FREQ = float(np.float32(10000.0) ** np.float32(-0.5))
TWO_PI_HI = 6.28125
TWO_PI_MID = float(np.float32(2 * np.pi - 6.28125) - np.float32(2 * np.pi - 6.28125) % np.float32(2.0 ** -21))
TWO_PI_LO = float(2 * np.pi - 6.28125 - TWO_PI_MID)
SIN_LIMIT = 3.1415925

S_NORM, S_PROJ, S_STACK, S_MAX, S_ATT, S_OUT, S_FFN = range(7)
STEPS = BATCH + S_FFN
LOOP_FROM, LOOP_TO = S_FFN + 2, BATCH
NEG_ROW = 24
VREG = 3


class Step:

    def __init__(self, it, s, looped, held=None):
        self.it, self.s, self.looped = it, s, looped
        self.held = {} if held is None else held

    def value(self, per_turn, at):
        return self.held.get((per_turn, at), per_turn * self.it + at)

    def hold(self, eng, stage, per, k):
        if self.looped:
            key = (2 * per, per * (self.s - stage) + k)
            if key not in self.held:
                reg = eng.alloc_register()
                eng.reg_add(reg, key[0] * self.it, key[1])
                self.held[key] = eng.snap(reg)

    def has(self, stage):
        return self.looped or 0 <= self.s - stage < BATCH

    def ring(self, stage):
        return (self.s - stage) % 2

    def batch(self, stage):
        return self.value(2, self.s - stage) if self.looped else self.s - stage

    def wait(self, eng, sem, stage, per, k):
        at = per * (self.s - stage) + k
        if self.looped:
            assert at > 0
            eng.wait_ge(sem, self.value(2 * per, at))
        elif at > 0:
            eng.wait_ge(sem, at)

    def wait_dma(self, eng, sems, stage, per, back=0):
        sem = sems[self.ring(stage)]
        at = per * ((self.s - stage) // 2 + 1 - back)
        if self.looped:
            assert at > 0
            eng.wait_ge(sem, self.value(per, at))
        elif at > 0:
            eng.wait_ge(sem, at)


def run_steps(eng, body, hold=None):
    for s in range(LOOP_FROM):
        body(Step(0, s, False))
    with eng.Fori(0, (LOOP_TO - LOOP_FROM) // 2) as it:
        held = {}
        turn = [Step(it, LOOP_FROM + u, True, held) for u in range(2)]
        if hold:
            for st in turn:
                hold(st)
        for st in turn:
            body(st)
    for s in range(LOOP_TO, STEPS):
        body(Step(0, s, False))


def bcast(ap, axis, n):
    ap = ap.unsqueeze(axis)
    shape = list(ap.shape)
    shape[axis] = n
    return ap.broadcast_to(shape)


def xattn_ffn_kernel(nc, x, ctx_in, pos, wq_d, wkv_d, wout_d, bout_d, w1_d, b1_d, w2_d, b2_d, s1_d, s2_d, out_d):
    stack = ExitStack()
    with stack:
        def sb(name, shape, dt=F32):
            return stack.enter_context(nc.sbuf_tensor(name, shape, dt))

        def sem(name):
            return stack.enter_context(nc.semaphore(name))

        def sems(name, n=2):
            return [sem(f"{name}{i}") for i in range(n)]

        ident = sb("ident", [128, 128])
        ident_bf = sb("ident_bf", [128, 128], BF16)
        zeros = sb("zeros", [128, HD])
        minus_half = sb("minus_half", [128, 1])
        wq = sb("wq", [128, DC, DIM])
        wkv = sb("wkv", [128, 2 * DIM])
        wout = sb("wout", [128, DC, DIM])
        bout = sb("bout", [128, DIM])
        b2 = sb("b2", [128, DIM])
        b2i = sb("b2i", [128, DIM], I32)
        b2q = sb("b2q", [128, DIM])
        b1 = sb("b1", [128, FC])
        b1i = sb("b1i", [128, FC], I32)
        b1q = sb("b1q", [128, FC])
        w1 = sb("w1", [128, FC, DIM])
        w2 = sb("w2", [128, DC, FFN])
        w_i = [sb("w1_i", [128, 2048], I16), sb("w2_i", [128, 2048], I16)]
        w_q = [sb("w1_q", [128, 2048], BF16), sb("w2_q", [128, 2048], BF16)]
        w1T = sb("w1T", [128, DC, FC, 128], BF16)
        w2T = sb("w2T", [128, FC, DIM], BF16)
        s_act = sb("s_act", [128, 2])
        r_act = sb("r_act", [128, 2])
        wmax = sb("wmax", [128, 2])
        wmax_all = sb("wmax_all", [128, 2])
        r_wmax = sb("r_wmax", [128, 2])
        w_levels = sb("w_levels", [128, 2])
        w_scale = sb("w_scale", [128, 2])
        h_scale = sb("h_scale", [128, 2])
        r_h_scale = sb("r_h_scale", [128, 2])
        relu_scale = sb("relu_scale", [128, 1])
        n_ang = BATCH * 4
        pos_sb = sb("pos_sb", [128, BATCH, 2])
        ang = sb("ang", [128, BATCH, 2, 2])
        turns = sb("turns", [128, 2, n_ang], I32)
        red = sb("red", [128, 4, 2, n_ang])
        trig = sb("trig", [128, 2, n_ang])
        cos8 = sb("cos8", [128, BATCH, 4, 2])
        sin_neg = sb("sin_neg", [128, BATCH, 4])
        sin_pos = sb("sin_pos", [128, BATCH, 4])
        x_ln = sb("x_ln", [128, 2, DIM])
        c_in = sb("c_in", [128, 2, CTX])
        x_res = sb("x_res", [128, 2, DIM])
        bn1 = sb("bn1", [128, 2, 6])
        mv1 = sb("mv1", [128, 2, 2])
        var1 = sb("var1", [128, 2, 1])
        rstd1 = sb("rstd1", [128, 2, 1])
        xn = sb("xn", [128, 2, DIM])
        xT = sb("xT", [128, 2, DIM + CTX])
        by_cos = sb("by_cos", [128, 2, 2 * DIM])
        by_sin = sb("by_sin", [128, 2, 2 * DIM])
        rot = sb("rot", [128, 2, 2 * DIM])
        q_rows = sb("q_rows", [128, 2, HEADS, 32])
        k_rows = sb("k_rows", [128, 2, HEADS, 32])
        q_comp = sb("q_comp", [128, 2, GROUPS, 128], F32R)
        k_stack = sb("k_stack", [128, 2, GROUPS, 128], F32R)
        q_diag = sb("q_diag", [128, 2, GROUPS, 512], F32R)
        v_comp = sb("v_comp", [128, 2, DIM])
        v_strip = sb("v_strip", [128, 2, HEADS, 32])
        mx = sb("mx", [128, 2, HEADS])
        mxT = sb("mxT", [16, 2, 2, 128], F32R)
        expo = sb("expo", [128, 2, 512])
        av = sb("av", [128, 2, 384])
        r_sum = sb("r_sum", [128, 2, HEADS])
        attn = sb("attn", [128, 2, DIM])
        attnT = sb("attnT", [128, 2, DIM])
        x_b = sb("x_b", [128, 2, DIM])
        x2 = sb("x2", [128, 2, DIM])
        bn2 = sb("bn2", [128, 2, 6])
        mv2 = sb("mv2", [128, 2, 2])
        var2 = sb("var2", [128, 2, 1])
        rstd2 = sb("rstd2", [128, 2, 1])
        xn2 = sb("xn2", [128, 2, DIM])
        xq_i = sb("xq_i", [128, 2, DIM], I16)
        xq = sb("xq", [128, 2, DIM], BF16)
        xqT = sb("xqT", [128, 2, DIM], BF16)
        h_i = sb("h_i", [128, 2, FC, 128], I16)
        hq = sb("hq", [128, 2, FC, 128], BF16)
        x2_b = sb("x2_b", [128, 2, DIM])
        y = sb("y", [128, 2, DIM])

        def bank(name):
            return stack.enter_context(nc.psum_tensor(name, [128, 512], F32))

        ps_max = [bank("ps_max0"), bank("ps_max1")]
        ps_exp = [bank("ps_exp0"), bank("ps_exp1")]
        ps_av01 = bank("ps_av01")
        ps_av2 = bank("ps_av2")
        ps_misc = [bank("ps_misc0"), bank("ps_misc1")]

        x_loaded = sems("x_loaded")
        res_loaded = sems("res_loaded")
        stored = sems("stored")
        early_loaded = sem("early_loaded")
        late_loaded = sem("late_loaded")
        diag_placed = [sems("diag_placed_lo"), sems("diag_placed_hi")]
        neg_placed = [sems("neg_placed_lo"), sems("neg_placed_hi")]
        id_ready = sem("id_ready")
        rope_step = sem("rope_step")
        ang_ready = sem("ang_ready")
        trig_ready = sem("trig_ready")
        wprep = sem("wprep")
        wmax_ready = sem("wmax_ready")
        wmax_shared = sem("wmax_shared")
        wq_ready = sem("wq_ready")
        wT_in_psum = sem("wT_in_psum")
        wT_ready = sems("wT_ready")
        pads_ready = sem("pads_ready")
        zeros_ready = sem("zeros_ready")
        ident_bf_ready = sem("ident_bf_ready")
        ln1_step = sem("ln1_step")
        var1_ready = sem("var1_ready")
        rstd1_ready = sem("rstd1_ready")
        xn_ready = sem("xn_ready")
        xT_in_psum = sem("xT_in_psum")
        xT_ready = sem("xT_ready")
        qk_in_psum = sem("qk_in_psum")
        rope_terms = sem("rope_terms")
        rot_ready = sem("rot_ready")
        hi_ready = sem("hi_ready")
        lo_ready = sem("lo_ready")
        v_in_psum = sem("v_in_psum")
        v_copied = sem("v_copied")
        v_ready = sem("v_ready")
        q_in_psum = sem("q_in_psum")
        q_ready = sem("q_ready")
        k_in_psum = sem("k_in_psum")
        k_ready = sem("k_ready")
        max_scores = sem("max_scores")
        max_done = sem("max_done")
        mx_in_psum = sem("mx_in_psum")
        mxT_ready = sem("mxT_ready")
        exp_scores = sem("exp_scores")
        exp_done = sem("exp_done")
        av_done = sem("av_done")
        av01_copied = sem("av01_copied")
        av2_copied = sem("av2_copied")
        attn_in_psum = sem("attn_in_psum")
        r_sum_ready = sem("r_sum_ready")
        attn_ready = sem("attn_ready")
        attnT_in_psum = sem("attnT_in_psum")
        attnT_ready = sem("attnT_ready")
        wo_in_psum = sem("wo_in_psum")
        x_b_ready = sem("x_b_ready")
        x2_ready = sem("x2_ready")
        ln2_step = sem("ln2_step")
        var2_ready = sem("var2_ready")
        rstd2_ready = sem("rstd2_ready")
        xq_step = sem("xq_step")
        xq_ready = sem("xq_ready")
        xqT_in_psum = sem("xqT_in_psum")
        xqT_ready = sem("xqT_ready")
        h_in_psum = sem("h_in_psum")
        relu_done = sem("relu_done")
        hq_ready = sem("hq_ready")
        y_in_psum = sem("y_in_psum")
        x2_b_ready = sem("x2_b_ready")
        y_ready = sem("y_ready")

        block = stack.enter_context(nc.Block())

        def copy_wT(eng, n):
            src = ps_misc[n % 2][:, 0:256].bitcast(BF16).rearrange("p (f c) -> p f c", f=4)
            which, c, quarter = n // 4, n // 2 % 2, n % 2
            fs = slice(4 * quarter, 4 * quarter + 4)
            dst = w1T[:, c, fs, :] if which == 0 else w2T[:, fs, 128 * c:128 * c + 128]
            return eng.tensor_copy(dst, src) if eng is nc.vector else eng.copy(dst, src)

        def copy_weights(eng, bank_n):
            for n in range(bank_n, 8, 2):
                eng.wait_ge(wT_in_psum, n + 1)
                copy_wT(eng, n).then_inc(wT_ready[bank_n], 1)

        def all_rows(ap):
            return bcast(ap, 0, 128)

        @block.sync
        def _(sp):
            def load(st):
                r, b = st.ring(S_NORM), st.batch(S_NORM)
                st.wait(sp, xn_ready, S_NORM, 1, -1)
                sp.dma_start(x_ln[:, r, :], x[b]).then_inc(x_loaded[r], 16)
                st.wait(sp, xT_in_psum, S_NORM, 1, -1)
                sp.dma_start(c_in[:, r, :], ctx_in[b]).then_inc(x_loaded[r], 16)

            def load_residual(st):
                r, b = st.ring(S_ATT), st.batch(S_ATT)
                st.wait(sp, x_b_ready, S_ATT, 1, -1)
                sp.dma_start(x_res[:, r, :], x[b]).then_inc(res_loaded[r], 16)

            def place_queries(st, half):
                r = st.ring(S_STACK)
                gs = slice(4 * half, 4 * half + 4)
                st.wait(sp, q_ready, S_STACK, 2, half + 1)
                st.wait(sp, exp_scores, S_STACK, GROUPS, 4 * half + 4 - 2 * GROUPS)
                if not st.looped and st.s == S_STACK:
                    sp.wait_ge(zeros_ready, 2)
                for j in range(4):
                    rows, cols = slice(32 * j, 32 * j + 32), slice(128 * j, 128 * j + 128)
                    sp.dma_start(q_diag[rows, r, gs, cols].bitcast(F32), q_comp[rows, r, gs, :].bitcast(F32))\
                      .then_inc(diag_placed[half][r], 16)

            def place_maxima(st, half, stage):
                r = st.ring(stage)
                st.wait(sp, mxT_ready, stage, 2, half + 1)
                for j in range(4):
                    row = 32 * j + NEG_ROW
                    dst = q_diag[row:row + 1, r, 4 * half:4 * half + 4, 128 * j:128 * j + 128]
                    sp.dma_start(dst.bitcast(F32), mxT[j:13 + j:4, r, half, :].bitcast(F32))\
                      .then_inc(neg_placed[half][r], 16)

            def store(st):
                r, b = st.ring(S_FFN), st.batch(S_FFN)
                st.wait(sp, y_ready, S_FFN, 1, 1)
                sp.dma_start(out_d[b], y[:, r, :]).then_inc(stored[r], 16)

            def body(st):
                if st.has(S_NORM):
                    load(st)
                if st.has(S_ATT):
                    load_residual(st)
                    place_maxima(st, 1, S_ATT)
                if st.has(S_STACK):
                    place_queries(st, 0)
                if st.has(S_MAX):
                    place_maxima(st, 0, S_MAX)
                if st.has(S_STACK):
                    place_queries(st, 1)
                if st.has(S_FFN):
                    store(st)
                if not st.looped and st.s == 0:
                    for c in range(DC):
                        sp.dma_start(wq[:, c, :], wq_d[128 * c:128 * c + 128, :]).then_inc(early_loaded, 16)
                    sp.dma_start(wkv[:, :], wkv_d).then_inc(early_loaded, 16)
                    late = [
                        (w1[:, :, :], w1_d.rearrange("(c p) d -> p c d", p=128)),
                        (w2[:, :, :], w2_d.rearrange("(c p) f -> p c f", p=128)),
                        (wout[:, :, :], wout_d.rearrange("(c p) d -> p c d", p=128)),
                        (b1[:, :], b1_d.rearrange("(c p) -> p c", p=128)),
                        (bout[:, :], all_rows(bout_d)),
                        (b2[:, :], all_rows(b2_d)),
                        (s_act[:, 0:1], all_rows(s1_d)),
                        (s_act[:, 1:2], all_rows(s2_d)),
                    ]
                    for dst, src in late:
                        sp.dma_start(dst, src, allow_slow_non_contiguous=True).then_inc(late_loaded, 16)

            def hold(st):
                for stage, per, k in ((S_STACK, GROUPS, 4 - 2 * GROUPS), (S_STACK, GROUPS, 8 - 2 * GROUPS)):
                    st.hold(sp, stage, per, k)

            run_steps(sp, body, hold)
            for r in range(2):
                sp.wait_ge(stored[r], 16 * BATCH // 2)

        LATE = 16 * 8
        EARLY = 16 * 3
        POS = sem("pos_loaded")

        @block.gpsimd
        def _(pool):
            pool.memset(ident[:, :], 0.0).then_inc(id_ready, 1)
            pool.wait_ge(id_ready, 1)
            pool.affine_select(out=ident[:, :], in_=ident[:, :], compare_op=ALU.not_equal, fill=1.0,
                               base=0, pattern=[[-1, 128]], channel_multiplier=1).then_inc(id_ready, 1)
            pool.memset(zeros[:, :], 0.0).then_inc(id_ready, 1)
            pool.memset(minus_half[:, :], -0.5).then_inc(id_ready, 1)
            pool.wait_ge(id_ready, 4)
            pool.memset(q_rows[:, :, :, :], 0.0).then_inc(pads_ready, 1)
            pool.memset(k_rows[:, :, :, :], 0.0).then_inc(pads_ready, 1)
            pool.wait_ge(pads_ready, 2)
            pool.memset(k_rows[:, :, :, NEG_ROW:NEG_ROW + 1], -1.0).then_inc(pads_ready, 1)

            def norm(st):
                r = st.ring(S_NORM)
                st.wait(pool, var1_ready, S_NORM, 1, 1)
                st.wait(pool, xn_ready, S_NORM, 1, -1)
                pool.tensor_tensor(rstd1[:, r, :], var1[:, r, :], minus_half[:, :], ALU.pow).then_inc(rstd1_ready, 1)

            def rotate(st):
                r = st.ring(S_PROJ)
                st.wait(pool, rope_terms, S_PROJ, 3, 3)
                st.wait(pool, hi_ready, S_PROJ, 2, -2)
                st.wait(pool, lo_ready, S_PROJ, 2, -2)
                pool.tensor_tensor(rot[:, r, :], by_cos[:, r, :], by_sin[:, r, :], ALU.add).then_inc(rot_ready, 1)

            def split_low(st):
                r = st.ring(S_PROJ)
                for n, (rows, at) in enumerate(((q_rows, 16), (k_rows, 8))):
                    st.wait(pool, hi_ready, S_PROJ, 2, n + 1)
                    src = rot[:, r, n * DIM:(n + 1) * DIM].rearrange("p (h d) -> p h d", d=HD)
                    pool.tensor_tensor(rows[:, r, :, at:at + HD], src, rows[:, r, :, 0:HD], ALU.subtract)\
                        .then_inc(lo_ready, 1)

            def place_values(st):
                r = st.ring(S_MAX)
                st.wait(pool, v_copied, S_MAX, 1, 1)
                st.wait(pool, av_done, S_MAX, GROUPS, -GROUPS)
                if not st.looped and st.s == S_MAX:
                    pool.wait_ge(zeros_ready, 2)
                for region in range(3):
                    n = min(VREG, GROUPS - VREG * region)
                    h = 4 * VREG * region
                    strips = v_strip[:, r, h:h + 4 * n, :].rearrange("p (s i) c -> p s i c", s=n)
                    for s in range(n):
                        vals = v_comp[:, r, (h + 4 * s) * HD:(h + 4 * s + 4) * HD].rearrange("p (i d) -> p i d", d=HD)
                        nothing = bcast(zeros[:, 0:HD], 1, 4)
                        ins = pool.tensor_tensor(strips[:, s, :, 9 * s:9 * s + HD], vals, nothing, ALU.add)
                ins.then_inc(v_ready, 1)

            def residual_bias(st):
                r = st.ring(S_ATT)
                st.wait_dma(pool, res_loaded, S_ATT, 16)
                st.wait(pool, x2_ready, S_ATT, 1, -1)
                pool.tensor_tensor(x_b[:, r, :], x_res[:, r, :], bout[:, :], ALU.add).then_inc(x_b_ready, 1)

            def norm2(st):
                r = st.ring(S_OUT)
                st.wait(pool, var2_ready, S_OUT, 1, 1)
                st.wait(pool, xq_ready, S_OUT, 1, -1)
                pool.tensor_tensor(rstd2[:, r, :], var2[:, r, :], minus_half[:, :], ALU.pow).then_inc(rstd2_ready, 1)

            def output_bias(st):
                r = st.ring(S_OUT)
                st.wait(pool, x2_ready, S_OUT, 1, 1)
                st.wait(pool, y_ready, S_OUT, 1, -1)
                pool.tensor_tensor(x2_b[:, r, :], x2[:, r, :], b2q[:, :], ALU.add).then_inc(x2_b_ready, 1)

            def body(st):
                if not st.looped and st.s == 2:
                    pool.wait_ge(wmax_ready, 2)
                    pool.partition_all_reduce(wmax_all[:, :], wmax[:, :], 128, MAX_OP)\
                        .then_inc(wmax_shared, 1)
                if not st.looped and st.s == 3:
                    pool.wait_ge(late_loaded, LATE)
                    pool.wait_ge(wprep, WPREP)
                if st.has(S_PROJ):
                    rotate(st)
                    split_low(st)
                if st.has(S_ATT):
                    residual_bias(st)
                if st.has(S_MAX):
                    place_values(st)
                if st.has(S_NORM):
                    norm(st)
                if st.has(S_OUT):
                    norm2(st)
                    output_bias(st)

            run_steps(pool, body)

        @block.scalar
        def _(act):
            act.dma_start(pos_sb[:, :, :], pos.rearrange("b t p -> t b p")).then_inc(POS, 16)
            act.wait_ge(id_ready, 2)
            act.copy(ident_bf[:, :], ident[:, :]).then_inc(ident_bf_ready, 1)
            act.wait_ge(ang_ready, 1)
            act.activation(trig[:, :, :], red[:, 3, :, :], ACT.Sin).then_inc(trig_ready, 1)

            def copy_xT(st):
                r = st.ring(S_PROJ)
                st.wait(act, xT_in_psum, S_PROJ, 1, 1)
                st.wait(act, v_in_psum, S_PROJ, 1, -1)
                act.copy(xT[:, r, :], ps_misc[XT % 2][:, 0:DIM + CTX]).then_inc(xT_ready, 1)

            def split_high(st):
                r = st.ring(S_PROJ)
                st.wait(act, rot_ready, S_PROJ, 1, 1)
                if not st.looped and st.s == S_PROJ:
                    act.wait_ge(pads_ready, 3)
                st.wait(act, q_in_psum, S_PROJ, 2, -2)
                q = bcast(rot[:, r, 0:DIM].rearrange("p (h d) -> p h d", d=HD), 2, 2)
                q_out = q_rows[:, r, :, 0:2 * HD].bitcast(F32R).rearrange("p h (c d) -> p h c d", d=HD)
                act.copy(q_out, q).then_inc(hi_ready, 1)
                st.wait(act, k_in_psum, S_PROJ, 2, -2)
                k = bcast(rot[:, r, DIM:2 * DIM].rearrange("p (h d) -> p h d", d=HD), 2, 2)
                k_out = k_rows[:, r, :, :].bitcast(F32R).rearrange("p h (c d) -> p h c d", d=HD)[:, :, 0:3:2, :]
                act.copy(k_out, k).then_inc(hi_ready, 1)

            def copy_v(st):
                r = st.ring(S_PROJ)
                st.wait(act, v_in_psum, S_PROJ, 1, 1)
                st.wait(act, v_ready, S_PROJ, 1, -1)
                act.copy(v_comp[:, r, :], ps_misc[VV % 2][:, 0:DIM]).then_inc(v_copied, 1)

            def copy_keys(st, half):
                r = st.ring(S_STACK)
                st.wait(act, k_in_psum, S_STACK, 2, half + 1)
                st.wait(act, exp_scores, S_STACK, GROUPS, 4 * half + 4 - 2 * GROUPS)
                act.copy(k_stack[:, r, 4 * half:4 * half + 4, :],
                         ps_misc[(SK0, SK1)[half] % 2][:, :].rearrange("p (g t) -> p g t", g=4)).then_inc(k_ready, 1)

            def exponentials(st, g):
                st.wait(act, exp_scores, S_ATT, GROUPS, g + 1)
                st.wait(act, av_done, S_ATT, GROUPS, g - 1)
                act.activation(expo[:, g % 2, :], ps_exp[g % 2][:, :], ACT.Exp, scale=SCALE).then_inc(exp_done, 1)

            def copy_av01(st):
                r = st.ring(S_ATT)
                st.wait(act, av_done, S_ATT, GROUPS, 2 * VREG)
                st.wait(act, attn_in_psum, S_ATT, 1, -1)
                act.copy(av[:, r, 0:256], ps_av01[:, 0:256]).then_inc(av01_copied, 1)

            def copy_av2(st):
                r = st.ring(S_OUT)
                st.wait(act, av_done, S_OUT, GROUPS, GROUPS)
                act.copy(av[:, r, 256:384], ps_av2[:, 0:128]).then_inc(av2_copied, 1)

            def copy_attnT(st):
                r = st.ring(S_OUT)
                st.wait(act, attnT_in_psum, S_OUT, 1, 1)
                st.wait(act, wo_in_psum, S_OUT, 1, -1)
                act.copy(attnT[:, r, :], ps_misc[AT2 % 2][:, 0:DIM]).then_inc(attnT_ready, 1)

            def copy_xqT(st):
                r = st.ring(S_FFN)
                st.wait(act, xqT_in_psum, S_FFN, 1, 1)
                st.wait(act, h_in_psum, S_FFN, 2, -2)
                act.copy(xqT[:, r, :], ps_misc[XQ % 2][:, 0:DIM // 2].bitcast(BF16)).then_inc(xqT_ready, 1)

            def relu(st, half):
                r = st.ring(S_FFN)
                st.wait(act, h_in_psum, S_FFN, 2, half + 1)
                st.wait(act, hq_ready, S_FFN, 2, half - 3)
                if not st.looped and st.s == S_FFN and half == 0:
                    act.wait_ge(wprep, WPREP)
                for c in range(4):
                    f = 4 * half + c
                    ins = act.activation(h_i[:, r, f, :], ps_misc[(H0, H1)[half] % 2][:, 128 * c:128 * c + 128],
                                         ACT.Relu, bias=b1q[:, f:f + 1], scale=relu_scale[:, :])
                ins.then_inc(relu_done, 1)

            def body(st):
                if not st.looped and st.s == 3:
                    copy_weights(act, 1)
                for g in range(GROUPS):
                    if st.has(S_ATT):
                        exponentials(st, g)
                    if g == 0 and st.has(S_OUT):
                        copy_av2(st)
                    if g == 0 and st.has(S_PROJ):
                        copy_xT(st)
                    if g == 2 and st.has(S_FFN):
                        copy_xqT(st)
                    if g == 3 and st.has(S_PROJ):
                        split_high(st)
                    if g == 4 and st.has(S_FFN):
                        relu(st, 0)
                    if g == 4 and st.has(S_OUT):
                        copy_attnT(st)
                    if g == 5 and st.has(S_FFN):
                        relu(st, 1)
                    if g == 6 and st.has(S_ATT):
                        copy_av01(st)
                    if g == 6 and st.has(S_PROJ):
                        copy_v(st)
                    if g == 6 and st.has(S_STACK):
                        copy_keys(st, 0)
                    if g == 7 and st.has(S_STACK):
                        copy_keys(st, 1)

            run_steps(act, body)

        @block.vector
        def _(dve):
            steps = [0]

            def link(ins, chain):
                steps[0] += 1
                ins.then_inc(chain, 1)
                dve.wait_ge(chain, steps[0])

            dve.memset(q_diag[:, :, :, :].bitcast(I32), 0)
            dve.memset(v_strip[:, :, :, :], 0.0).then_inc(zeros_ready, 1)
            dve.wait_ge(zeros_ready, 1)
            for s in range(VREG):
                for g in range(s, GROUPS, VREG):
                    ins = dve.memset(v_strip[:, :, 4 * g:4 * g + 4, 9 * s + HD:9 * s + HD + 1], 1.0)
            ins.then_inc(zeros_ready, 1)

            dve.wait_ge(POS, 16)
            for f, freq in enumerate((1.0, ROPE_FREQ)):
                link(dve.tensor_scalar(ang[:, :, :, f], pos_sb[:, :, :], freq, None, ALU.mult), rope_step)
            angles = ang[:, :, :, :].rearrange("p b a f -> p (b a f)")
            for n in range(2):
                link(dve.tensor_scalar(turns[:, n, :], angles, 1.0 / (2 * np.pi), 0.25 * n, ALU.mult, ALU.add), rope_step)
                link(dve.tensor_copy(red[:, 0, n, :], turns[:, n, :]), rope_step)
                link(dve.scalar_tensor_tensor(out=red[:, 1, n, :], in0=red[:, 0, n, :], scalar=-TWO_PI_HI, in1=angles,
                                              op0=ALU.mult, op1=ALU.add), rope_step)
                link(dve.scalar_tensor_tensor(out=red[:, 2, n, :], in0=red[:, 0, n, :], scalar=-TWO_PI_MID,
                                              in1=red[:, 1, n, :], op0=ALU.mult, op1=ALU.add), rope_step)
                link(dve.scalar_tensor_tensor(out=red[:, 1, n, :], in0=red[:, 0, n, :], scalar=-TWO_PI_LO,
                                              in1=red[:, 2, n, :], op0=ALU.mult, op1=ALU.add), rope_step)
                link(dve.tensor_scalar(red[:, 2, n, :], red[:, 1, n, :], 0.5 * np.pi * n, SIN_LIMIT, ALU.add, ALU.min),
                     rope_step)
                link(dve.tensor_scalar(red[:, 3, n, :], red[:, 2, n, :], -SIN_LIMIT, None, ALU.max), rope_step)
            dve.wait_ge(rope_step, steps[0])
            dve.tensor_copy(red[:, 0, 0, 0:1], red[:, 3, 0, 0:1]).then_inc(ang_ready, 1)
            dve.wait_ge(trig_ready, 1)
            sine = trig[:, 0, :].rearrange("p (b f) -> p b f", b=BATCH)
            cosine = trig[:, 1, :].rearrange("p (b f) -> p b f", b=BATCH)
            dve.tensor_copy(cos8[:, :, :, 0], cosine)
            dve.tensor_copy(cos8[:, :, :, 1], cosine)
            dve.tensor_scalar(sin_neg[:, :, :], sine, -1.0, None, ALU.mult)
            link(dve.tensor_copy(sin_pos[:, :, :], sine), rope_step)

            def prepare_weights():
                steps[0] = 0
                views = [w1[:, :, :].rearrange("p c d -> p (c d)"), w2[:, :, :].rearrange("p c f -> p (c f)")]
                for n in range(2):
                    dve.tensor_reduce(out=wmax[:, n:n + 1], in_=views[n], axis=AX.X, op=ALU.max,
                                      apply_absolute_value=True).then_inc(wmax_ready, 1)
                link(dve.reciprocal(r_act[:, :], s_act[:, :]), wprep)
                dve.wait_ge(wmax_shared, 1)
                link(dve.reciprocal(r_wmax[:, :], wmax_all[:, :]), wprep)
                link(dve.tensor_scalar(w_levels[:, :], r_wmax[:, :], QMAX, None, ALU.mult), wprep)
                for n in range(2):
                    link(dve.tensor_scalar(w_i[n][:, :], views[n], w_levels[:, n:n + 1], None, ALU.mult), wprep)
                    dve.tensor_scalar(w_q[n][:, :], w_i[n][:, :], QMIN, QMAX, ALU.max, ALU.min).then_inc(wq_ready, 1)
                link(dve.tensor_scalar(w_scale[:, :], wmax_all[:, :], 1.0 / QMAX, None, ALU.mult), wprep)
                link(dve.tensor_tensor(h_scale[:, :], w_scale[:, :], s_act[:, :], ALU.mult), wprep)
                link(dve.reciprocal(r_h_scale[:, :], h_scale[:, :]), wprep)
                link(dve.tensor_tensor(relu_scale[:, :], h_scale[:, 0:1], r_act[:, 1:2], ALU.mult), wprep)
                link(dve.tensor_scalar(b1i[:, :], b1[:, :], r_h_scale[:, 0:1], None, ALU.mult), wprep)
                link(dve.tensor_scalar(b1q[:, :], b1i[:, :], relu_scale[:, :], None, ALU.mult), wprep)
                link(dve.tensor_scalar(b2i[:, :], b2[:, :], r_h_scale[:, 1:2], None, ALU.mult), wprep)
                link(dve.tensor_scalar(b2q[:, :], b2i[:, :], h_scale[:, 1:2], None, ALU.mult), wprep)
                assert steps[0] == WPREP

            def norm1_stats(st):
                r = st.ring(S_NORM)
                st.wait_dma(dve, x_loaded, S_NORM, 32)
                dve.bn_stats(bn1[:, r, :], x_ln[:, r, :]).then_inc(ln1_step, 1)

            def norm1_moments(st):
                r = st.ring(S_NORM)
                dve.bn_aggr(mv1[:, r, :], bn1[:, r, :]).then_inc(ln1_step, 1)
                st.wait(dve, ln1_step, S_NORM, 2, 2)
                st.wait(dve, rstd1_ready, S_NORM, 1, -1)
                dve.tensor_scalar(var1[:, r, :], mv1[:, r, 1:2], EPS, None, ALU.add).then_inc(var1_ready, 1)

            def norm1(st):
                r = st.ring(S_NORM)
                st.wait(dve, rstd1_ready, S_NORM, 1, 1)
                st.wait(dve, xT_in_psum, S_NORM, 1, -1)
                dve.tensor_scalar(xn[:, r, :], x_ln[:, r, :], mv1[:, r, 0:1], rstd1[:, r, :],
                                  ALU.subtract, ALU.mult).then_inc(xn_ready, 1)

            def rope(st):
                r, b = st.ring(S_PROJ), st.batch(S_PROJ)
                st.wait(dve, qk_in_psum, S_PROJ, 1, 1)
                st.wait(dve, rot_ready, S_PROJ, 1, -1)
                ps = ps_misc[QK % 2][:, :]
                cos_b = bcast(cos8[:, b, :, :].rearrange("p f c -> p (f c)"), 1, 2 * HEADS)
                dve.tensor_tensor(by_cos[:, r, :].rearrange("p (h d) -> p h d", d=HD),
                                  ps.rearrange("p (h d) -> p h d", d=HD), cos_b, ALU.mult).then_inc(rope_terms, 1)
                pairs_in = ps.rearrange("p (h f c) -> p h f c", f=4, c=2)
                pairs_out = by_sin[:, r, :].rearrange("p (h f c) -> p h f c", f=4, c=2)
                for c, s in enumerate((sin_neg, sin_pos)):
                    dve.tensor_tensor(pairs_out[:, :, :, c], pairs_in[:, :, :, 1 - c],
                                      bcast(s[:, b, :], 1, 2 * HEADS), ALU.mult).then_inc(rope_terms, 1)

            def copy_queries(st, half):
                r = st.ring(S_STACK)
                st.wait(dve, q_in_psum, S_STACK, 2, half + 1)
                st.wait_dma(dve, diag_placed[half], S_STACK, 64, back=1)
                dve.tensor_copy(q_comp[:, r, 4 * half:4 * half + 4, :],
                                ps_misc[(SQ0, SQ1)[half] % 2][:, :].rearrange("p (g t) -> p g t", g=4))\
                   .then_inc(q_ready, 1)

            def maxima(st, g):
                r = st.ring(S_MAX)
                st.wait(dve, max_scores, S_MAX, GROUPS, g + 1)
                if g == 0:
                    st.wait(dve, mx_in_psum, S_MAX, 2, -2)
                dve.tensor_reduce(out=mx[:, r, 4 * g:4 * g + 4],
                                  in_=ps_max[g % 2][:, :].rearrange("p (h k) -> p h k", h=4),
                                  axis=AX.X, op=ALU.max).then_inc(max_done, 1)

            def copy_maxima(st, half, stage):
                r = st.ring(stage)
                st.wait(dve, mx_in_psum, stage, 2, half + 1)
                st.wait_dma(dve, neg_placed[half], stage, 64, back=1)
                dve.tensor_copy(mxT[:, r, half, :], ps_misc[(MX0, MX1)[half] % 2][0:16, 0:128]).then_inc(mxT_ready, 1)

            def normalise(st):
                r = st.ring(S_OUT)
                st.wait(dve, attn_in_psum, S_OUT, 1, 1)
                st.wait(dve, attn_ready, S_OUT, 1, -1)
                st.wait(dve, attnT_in_psum, S_OUT, 1, -1)
                for region in range(3):
                    n = min(VREG, GROUPS - VREG * region)
                    cols = ps_misc[AT1 % 2][:, 128 * region:128 * region + 128].rearrange("p (i c) -> p i c", i=4)
                    sums = cols[:, :, 0:9 * n].rearrange("p i (s d) -> p s i d", d=9)[:, :, :, HD:HD + 1]
                    h = 4 * VREG * region
                    ins = dve.reciprocal(r_sum[:, r, h:h + 4 * n].rearrange("p (s i d) -> p s i d", s=n, d=1), sums)
                ins.then_inc(r_sum_ready, 1)
                st.wait(dve, r_sum_ready, S_OUT, 1, 1)
                for region in range(3):
                    n = min(VREG, GROUPS - VREG * region)
                    cols = ps_misc[AT1 % 2][:, 128 * region:128 * region + 128].rearrange("p (i c) -> p i c", i=4)
                    vals = cols[:, :, 0:9 * n].rearrange("p i (s d) -> p s i d", d=9)[:, :, :, 0:HD]
                    h = 4 * VREG * region
                    scale = bcast(r_sum[:, r, h:h + 4 * n].rearrange("p (s i) -> p s i", s=n), 3, HD)
                    dst = attn[:, r, h * HD:(h + 4 * n) * HD].rearrange("p (s i d) -> p s i d", s=n, d=HD)
                    ins = dve.tensor_tensor(dst, vals, scale, ALU.mult)
                ins.then_inc(attn_ready, 1)

            def residual(st):
                r = st.ring(S_OUT)
                st.wait(dve, wo_in_psum, S_OUT, 1, 1)
                st.wait(dve, x_b_ready, S_OUT, 1, 1)
                st.wait(dve, x2_b_ready, S_OUT, 1, -1)
                dve.tensor_tensor(x2[:, r, :], ps_misc[WO % 2][:, 0:DIM], x_b[:, r, :], ALU.add).then_inc(x2_ready, 1)
                st.wait(dve, x2_ready, S_OUT, 1, 1)
                dve.bn_stats(bn2[:, r, :], x2[:, r, :]).then_inc(ln2_step, 1)

            def norm2_moments(st):
                r = st.ring(S_OUT)
                dve.bn_aggr(mv2[:, r, :], bn2[:, r, :]).then_inc(ln2_step, 1)
                st.wait(dve, ln2_step, S_OUT, 2, 2)
                st.wait(dve, rstd2_ready, S_OUT, 1, -1)
                dve.tensor_scalar(var2[:, r, :], mv2[:, r, 1:2], EPS, None, ALU.add).then_inc(var2_ready, 1)

            def quantise_x(st):
                r = st.ring(S_OUT)
                st.wait(dve, rstd2_ready, S_OUT, 1, 1)
                dve.tensor_scalar(xn2[:, r, :], x2[:, r, :], mv2[:, r, 0:1], rstd2[:, r, :],
                                  ALU.subtract, ALU.mult).then_inc(xq_step, 1)
                st.wait(dve, xq_step, S_OUT, 2, 1)
                dve.tensor_scalar(xq_i[:, r, :], xn2[:, r, :], r_act[:, 0:1], None, ALU.mult).then_inc(xq_step, 1)
                st.wait(dve, xq_step, S_OUT, 2, 2)
                st.wait(dve, xqT_in_psum, S_OUT, 1, -1)
                dve.tensor_scalar(xq[:, r, :], xq_i[:, r, :], QMIN, QMAX, ALU.max, ALU.min).then_inc(xq_ready, 1)

            def clip_h(st, half):
                r = st.ring(S_FFN)
                fs = slice(4 * half, 4 * half + 4)
                st.wait(dve, relu_done, S_FFN, 2, half + 1)
                st.wait(dve, y_in_psum, S_FFN, 1, -1)
                dve.tensor_scalar(hq[:, r, fs, :], h_i[:, r, fs, :], 0.0, HMAX, ALU.max, ALU.min).then_inc(hq_ready, 1)

            def output(st):
                r = st.ring(S_FFN)
                st.wait(dve, y_in_psum, S_FFN, 1, 1)
                st.wait(dve, x2_b_ready, S_FFN, 1, 1)
                st.wait_dma(dve, stored, S_FFN, 16, back=1)
                dve.scalar_tensor_tensor(out=y[:, r, :], in0=ps_misc[YY % 2][:, 0:DIM], scalar=h_scale[:, 1:2],
                                         in1=x2_b[:, r, :], op0=ALU.mult, op1=ALU.add).then_inc(y_ready, 1)

            def body(st):
                if not st.looped and st.s == 2:
                    dve.wait_ge(late_loaded, LATE)
                    prepare_weights()
                if not st.looped and st.s == 3:
                    copy_weights(dve, 0)
                for g in range(GROUPS):
                    if g == 5 and st.has(S_NORM):
                        st.wait(dve, ln1_step, S_NORM, 2, 1)
                    if g == 6 and st.has(S_OUT):
                        st.wait(dve, ln2_step, S_OUT, 2, 1)
                    if st.has(S_MAX):
                        maxima(st, g)
                    if g == 4 and st.has(S_NORM):
                        norm1_stats(st)
                    if g == 5 and st.has(S_NORM):
                        norm1_moments(st)
                    if g == 6 and st.has(S_OUT):
                        norm2_moments(st)
                    if g == 0 and st.has(S_STACK):
                        copy_queries(st, 0)
                    if g == 1 and st.has(S_ATT):
                        copy_maxima(st, 1, S_ATT)
                    if g == 1 and st.has(S_PROJ):
                        rope(st)
                    if g == 2 and st.has(S_OUT):
                        normalise(st)
                    if g == 3 and st.has(S_STACK):
                        copy_queries(st, 1)
                    if g == 5 and st.has(S_FFN):
                        clip_h(st, 0)
                    if g == 5 and st.has(S_OUT):
                        residual(st)
                    if g == 5 and st.has(S_MAX):
                        copy_maxima(st, 0, S_MAX)
                    if g == 6 and st.has(S_FFN):
                        clip_h(st, 1)
                    if g == 6 and st.has(S_NORM):
                        norm1(st)
                    if g == 7 and st.has(S_OUT):
                        quantise_x(st)
                    if g == 7 and st.has(S_FFN):
                        output(st)

            run_steps(dve, body)

        @block.tensor
        def _(pe):
            def mm(out, lhsT, rhs, start=True, stop=True, **kw):
                return pe.matmul(out, lhsT, rhs, start=start, stop=stop, skip_group_check=True, **kw)

            def transpose(out, in_, idn):
                return mm(out, in_, idn, is_transpose=True)

            emptied = {
                XT: (xT_ready, S_PROJ, 1, 1), SQ0: (q_ready, S_STACK, 2, 1), MX1: (mxT_ready, S_ATT, 2, 2),
                QK: (rope_terms, S_PROJ, 3, 3), AT1: (attn_ready, S_OUT, 1, 1), XQ: (xqT_ready, S_FFN, 1, 1),
                SQ1: (q_ready, S_STACK, 2, 2), H0: (relu_done, S_FFN, 2, 1), AT2: (attnT_ready, S_OUT, 1, 1),
                H1: (relu_done, S_FFN, 2, 2), WO: (x2_ready, S_OUT, 1, 1), MX0: (mxT_ready, S_MAX, 2, 1),
                VV: (v_copied, S_PROJ, 1, 1), SK0: (k_ready, S_STACK, 2, 1), YY: (y_ready, S_FFN, 1, 1),
                SK1: (k_ready, S_STACK, 2, 2),
            }

            def claim(st, piece):
                p, prev = piece - 2, st
                for _ in range(2 * PIECES):
                    if p < 0:
                        p += PIECES
                        prev = Step(st.it, prev.s - 1, st.looped, st.held)
                    s_, stage, per, k = emptied[p]
                    if prev.has(stage):
                        prev.wait(pe, s_, stage, per, k)
                        return ps_misc[piece % 2]
                    p -= 2
                return ps_misc[piece % 2]

            def transpose_x(st):
                ps, r = claim(st, XT), st.ring(S_PROJ)
                st.wait(pe, xn_ready, S_PROJ, 1, 1)
                st.wait_dma(pe, x_loaded, S_PROJ, 32)
                for c in range(DC):
                    transpose(ps[:, 128 * c:128 * c + 128], xn[:, r, 128 * c:128 * c + 128], ident[:, :])
                transpose(ps[:, DIM:DIM + CTX], c_in[:, r, :], ident[:, :]).then_inc(xT_in_psum, 1)

            def project_qk(st):
                ps, r = claim(st, QK), st.ring(S_PROJ)
                st.wait(pe, xT_ready, S_PROJ, 1, 1)
                for c in range(DC):
                    mm(ps[:, 0:DIM], xT[:, r, 128 * c:128 * c + 128], wq[:, c, :], c == 0, c == DC - 1)
                mm(ps[:, DIM:2 * DIM], xT[:, r, DIM:DIM + CTX], wkv[:, 0:DIM]).then_inc(qk_in_psum, 1)

            def project_v(st):
                ps, r = claim(st, VV), st.ring(S_PROJ)
                mm(ps[:, 0:DIM], xT[:, r, DIM:DIM + CTX], wkv[:, DIM:2 * DIM]).then_inc(v_in_psum, 1)

            def transpose_rows(st, piece, rows, in_psum, ready, half):
                ps, r = claim(st, piece), st.ring(S_STACK)
                st.wait(pe, lo_ready, S_STACK, 2, ready)
                for g in range(4):
                    h = 4 * (4 * half + g)
                    ins = transpose(ps[:, 128 * g:128 * g + 128], rows[:, r, h:h + 4, :].rearrange("p h c -> p (h c)"),
                                    ident[:, :])
                ins.then_inc(in_psum, 1)

            def scores_for_max(st, g):
                r = st.ring(S_MAX)
                if g % 4 == 0:
                    st.wait_dma(pe, diag_placed[g // 4], S_MAX, 64)
                    st.wait(pe, k_ready, S_MAX, 2, g // 4 + 1)
                st.wait(pe, max_done, S_MAX, GROUPS, g - 1)
                keys = k_stack[:, r, g, :].bitcast(BF16).rearrange("p (t w) -> p t w", w=2)[:, :, 1]
                queries = q_diag[:, r, g, :].bitcast(BF16).rearrange("p (t w) -> p t w", w=2)[:, :, 1]
                for i in range(4):
                    ins = mm(ps_max[g % 2][:, 128 * i:128 * i + 128], queries[:, 128 * i:128 * i + 128], keys)
                ins.then_inc(max_scores, 1)

            def transpose_maxima(st, half, stage, piece):
                ps, r = claim(st, piece), st.ring(stage)
                st.wait(pe, max_done, stage, GROUPS, 4 * half + 4)
                transpose(ps[0:16, 0:128], mx[:, r, 16 * half:16 * half + 16], ident[:, :]).then_inc(mx_in_psum, 1)

            def scores_for_exp(st, g):
                r = st.ring(S_ATT)
                if g % 4 == 0:
                    st.wait_dma(pe, neg_placed[g // 4], S_ATT, 64)
                st.wait(pe, exp_done, S_ATT, GROUPS, g - 1)
                mm(ps_exp[g % 2][:, :], k_stack[:, r, g, :], q_diag[:, r, g, :]).then_inc(exp_scores, 1)

            def weigh_values(st, g, stage):
                r = st.ring(stage)
                st.wait(pe, exp_done, stage, GROUPS, g + 1)
                if g == 0:
                    st.wait(pe, v_ready, stage, 1, 1)
                    st.wait(pe, av01_copied, stage, 1, 0)
                if g == 2 * VREG:
                    st.wait(pe, av2_copied, stage, 1, 0)
                region = g // VREG
                ps = ps_av2[:, 0:128] if region == 2 else ps_av01[:, 128 * region:128 * region + 128]
                for i in range(4):
                    ins = mm(ps[32 * i:32 * i + 32, :], v_strip[:, r, 4 * g + i, :], expo[:, g % 2, 128 * i:128 * i + 128],
                             g % VREG == 0, g % VREG == VREG - 1 or g == GROUPS - 1)
                ins.then_inc(av_done, 1)

            def transpose_av(st):
                ps, r = claim(st, AT1), st.ring(S_OUT)
                st.wait(pe, av01_copied, S_OUT, 1, 1)
                st.wait(pe, av2_copied, S_OUT, 1, 1)
                for c in range(3):
                    ins = transpose(ps[:, 128 * c:128 * c + 128], av[:, r, 128 * c:128 * c + 128], ident[:, :])
                ins.then_inc(attn_in_psum, 1)

            def transpose_attn(st):
                ps, r = claim(st, AT2), st.ring(S_OUT)
                st.wait(pe, attn_ready, S_OUT, 1, 1)
                for c in range(DC):
                    ins = transpose(ps[:, 128 * c:128 * c + 128], attn[:, r, 128 * c:128 * c + 128], ident[:, :])
                ins.then_inc(attnT_in_psum, 1)

            def project_out(st):
                ps, r = claim(st, WO), st.ring(S_OUT)
                st.wait(pe, attnT_ready, S_OUT, 1, 1)
                for c in range(DC):
                    ins = mm(ps[:, 0:DIM], attnT[:, r, 128 * c:128 * c + 128], wout[:, c, :], c == 0, c == DC - 1)
                ins.then_inc(wo_in_psum, 1)

            def transpose_xq(st):
                ps, r = claim(st, XQ), st.ring(S_FFN)
                st.wait(pe, xq_ready, S_FFN, 1, 1)
                for c in range(DC):
                    ins = transpose(ps[:, 64 * c:64 * c + 64].bitcast(BF16), xq[:, r, 128 * c:128 * c + 128],
                                    ident_bf[:, :])
                ins.then_inc(xqT_in_psum, 1)

            def hidden(st, half, piece):
                ps, r = claim(st, piece), st.ring(S_FFN)
                st.wait(pe, xqT_ready, S_FFN, 1, 1)
                for f in range(4):
                    for c in range(DC):
                        ins = mm(ps[:, 128 * f:128 * f + 128], w1T[:, c, 4 * half + f, :],
                                 xqT[:, r, 128 * c:128 * c + 128], c == 0, c == DC - 1)
                ins.then_inc(h_in_psum, 1)

            def project_y(st):
                ps, r = claim(st, YY), st.ring(S_FFN)
                st.wait(pe, hq_ready, S_FFN, 2, 2)
                for f in range(FC):
                    ins = mm(ps[:, 0:DIM], hq[:, r, f, :], w2T[:, f, :], f == 0, f == FC - 1)
                ins.then_inc(y_in_psum, 1)

            def transpose_weights():
                for n in range(8):
                    which, c, quarter = n // 4, n // 2 % 2, n % 2
                    pe.wait_ge(wq_ready, which + 1)
                    if n >= 2:
                        pe.wait_ge(wT_ready[n % 2], n // 2)
                    ps = ps_misc[n % 2][:, 0:256].bitcast(BF16)
                    for f in range(4):
                        fc = 4 * quarter + f
                        at = fc * DIM + 128 * c if which == 0 else c * FFN + 128 * fc
                        ins = transpose(ps[:, 128 * f:128 * f + 128], w_q[which][:, at:at + 128], ident_bf[:, :])
                    ins.then_inc(wT_in_psum, 1)
                for n in range(2):
                    pe.wait_ge(wT_ready[n], 4)

            def body(st):
                if not st.looped and st.s == 0:
                    pe.wait_ge(id_ready, 2)
                    pe.wait_ge(ident_bf_ready, 1)
                    pe.wait_ge(early_loaded, EARLY)
                    pe.wait_ge(pads_ready, 3)
                    pe.wait_ge(zeros_ready, 2)
                if not st.looped and st.s == 3:
                    pe.wait_ge(v_copied, 2)
                    pe.wait_ge(k_ready, 2)
                    transpose_weights()
                for g in range(GROUPS):
                    if st.has(S_MAX):
                        scores_for_max(st, g)
                    if st.has(S_ATT):
                        scores_for_exp(st, g)
                    if g == 0 and st.has(S_PROJ):
                        transpose_x(st)
                    if g == 0 and st.has(S_STACK):
                        transpose_rows(st, SQ0, q_rows, q_in_psum, 1, 0)
                    if g == 1 and st.has(S_ATT):
                        transpose_maxima(st, 1, S_ATT, MX1)
                    if g == 1 and st.has(S_PROJ):
                        project_qk(st)
                    if g == 2 and st.has(S_OUT):
                        transpose_av(st)
                    if g == 2 and st.has(S_FFN):
                        transpose_xq(st)
                    if g == 3 and st.has(S_STACK):
                        transpose_rows(st, SQ1, q_rows, q_in_psum, 1, 1)
                    if g == 3 and st.has(S_FFN):
                        hidden(st, 0, H0)
                    if g == 4 and st.has(S_OUT):
                        transpose_attn(st)
                    if g == 4 and st.has(S_FFN):
                        hidden(st, 1, H1)
                    if g == 5 and st.has(S_OUT):
                        project_out(st)
                    if g == 5 and st.has(S_MAX):
                        transpose_maxima(st, 0, S_MAX, MX0)
                    if g == 6 and st.has(S_PROJ):
                        project_v(st)
                    if g == 6 and st.has(S_STACK):
                        transpose_rows(st, SK0, k_rows, k_in_psum, 2, 0)
                    if g == 7 and st.has(S_FFN):
                        project_y(st)
                    if g == 7 and st.has(S_STACK):
                        transpose_rows(st, SK1, k_rows, k_in_psum, 2, 1)
                    if g == 0 and st.has(S_OUT):
                        weigh_values(st, GROUPS - 1, S_OUT)
                    if g > 0 and st.has(S_ATT):
                        weigh_values(st, g - 1, S_ATT)

            run_steps(pe, body)


XT, SQ0, MX1, QK, AT1, XQ, SQ1, H0, AT2, H1, WO, MX0, VV, SK0, YY, SK1 = range(16)
PIECES = 16
WPREP = 13
MAX_OP = bass.bass_isa.ReduceOp.max

_INS = ['x', 'ctx_1024', 'fside_BxSx2_0', 'L0_xattn_Wq', 'L0_xattn_Wkv', 'L0_xattn_Wout', 'L0_xattn_bout',
        'L0_ffn_W1', 'L0_ffn_b1', 'L0_ffn_W2', 'L0_ffn_b2', 'L0_ffn_s_act1', 'L0_ffn_s_act2']


def kernel(**inputs):
    import numpy as _np
    import concourse.bacc as _bacc
    from concourse import mybir as _mybir
    from concourse.bass_utils import run_bass_kernel_spmd as _run

    nc = _bacc.Bacc("TRN2", target_bir_lowering=False, num_devices=1)
    arrays, args = {}, []
    for name in _INS:
        a = _np.ascontiguousarray(inputs[name])
        arrays[f"in_{name}_dram"] = a
        args.append(nc.dram_tensor(f"in_{name}_dram", a.shape, _mybir.dt.from_np(a.dtype), kind="ExternalInput").ap())
    args.append(nc.dram_tensor("out_dram", (BATCH, TOK, DIM), _mybir.dt.float32, kind="ExternalOutput").ap())
    xattn_ffn_kernel(nc, *args)
    r = _run(nc, [arrays], core_ids=[0])
    return r.results[0]["out_dram"]
```

```python
import numpy as np
import concourse.bass as bass
from concourse import mybir
from contextlib import ExitStack

F32 = mybir.dt.float32
F32R = mybir.dt.float32r
BF16 = mybir.dt.bfloat16
I16 = mybir.dt.int16
I32 = mybir.dt.int32
ALU = mybir.AluOpType
ACT = mybir.ActivationFunctionType
AX = mybir.AxisListType

BATCH, TOK, DIM, CTX, HEADS, FFN = 16, 128, 256, 128, 32, 1024
HD = DIM // HEADS
GROUPS = HEADS // 4
DC = DIM // 128
FC = FFN // 128
EPS = 1e-5
SCALE = 1.0 / float(np.sqrt(np.float32(HD)))
QMIN, QMAX, HMAX = -8.0, 7.0, 15.0
ROPE_FREQ = float(np.float32(10000.0) ** np.float32(-0.5))
TWO_PI_HI = 6.28125
TWO_PI_MID = float(np.float32(2 * np.pi - 6.28125) - np.float32(2 * np.pi - 6.28125) % np.float32(2.0 ** -21))
TWO_PI_LO = float(2 * np.pi - 6.28125 - TWO_PI_MID)
SIN_LIMIT = 3.1415925

S_NORM, S_PROJ, S_STACK, S_MAX, S_ATT, S_OUT, S_FFN = range(7)
STEPS = BATCH + S_FFN
LOOP_FROM, LOOP_TO = S_FFN + 2, BATCH
XT, SQ0, MX1, QK, SQ1, XQ, AT1, H0, H1, MX0, AT2, VV, WO, SK0, SK1, YY = range(16)
PIECES = 16
PIECE_BANK = (0, 1, 2, 0, 1, 2, 0, 2, 1, 0, 0, 2, 0, 1, 1, 2)
EXPO = 4
LAG = 2
LOADS = ((0, 1), (1, 2), (2, 4), (4, 8), (8, 16))
NEG_ROW = 96 + 3 * HD
VREG = 3


class Step:

    def __init__(self, it, s, looped, held=None):
        self.it, self.s, self.looped = it, s, looped
        self.held = {} if held is None else held

    def value(self, per_turn, at):
        return self.held.get((per_turn, at), per_turn * self.it + at)

    def hold(self, eng, stage, per, k):
        if self.looped:
            key = (2 * per, per * (self.s - stage) + k)
            if key not in self.held:
                reg = eng.alloc_register()
                eng.reg_add(reg, key[0] * self.it, key[1])
                self.held[key] = eng.snap(reg)

    def has(self, stage):
        return self.looped or 0 <= self.s - stage < BATCH

    def ring(self, stage):
        return (self.s - stage) % 2

    def batch(self, stage):
        return self.value(2, self.s - stage) if self.looped else self.s - stage

    def wait(self, eng, sem, stage, per, k):
        at = per * (self.s - stage) + k
        if self.looped:
            assert at > 0
            eng.wait_ge(sem, self.value(2 * per, at))
        elif at > 0:
            eng.wait_ge(sem, at)

    def wait_dma(self, eng, sems, stage, per, back=0):
        sem = sems[self.ring(stage)]
        at = per * ((self.s - stage) // 2 + 1 - back)
        if self.looped:
            assert at > 0
            eng.wait_ge(sem, self.value(per, at))
        elif at > 0:
            eng.wait_ge(sem, at)


def run_steps(eng, body, hold=None):
    for s in range(LOOP_FROM):
        body(Step(0, s, False))
    with eng.Fori(0, (LOOP_TO - LOOP_FROM) // 2) as it:
        held = {}
        turn = [Step(it, LOOP_FROM + u, True, held) for u in range(2)]
        if hold:
            for st in turn:
                hold(st)
        for st in turn:
            body(st)
    for s in range(LOOP_TO, STEPS):
        body(Step(0, s, False))


def bcast(ap, axis, n):
    ap = ap.unsqueeze(axis)
    shape = list(ap.shape)
    shape[axis] = n
    return ap.broadcast_to(shape)


def xattn_ffn_kernel(nc, x, ctx_in, pos, wq_d, wkv_d, wout_d, bout_d, w1_d, b1_d, w2_d, b2_d, s1_d, s2_d, out_d):
    stack = ExitStack()
    with stack:
        def sb(name, shape, dt=F32):
            return stack.enter_context(nc.sbuf_tensor(name, shape, dt))

        def sem(name):
            return stack.enter_context(nc.semaphore(name))

        def sems(name, n=2):
            return [sem(f"{name}{i}") for i in range(n)]

        ident = sb("ident", [128, 128])
        ident_bf = sb("ident_bf", [128, 128], BF16)
        zeros = sb("zeros", [128, HD])
        minus_half = sb("minus_half", [128, 1])
        wq = sb("wq", [128, DC, DIM])
        wkv = sb("wkv", [128, 2 * DIM])
        wout = sb("wout", [128, DC, DIM])
        bout = sb("bout", [128, DIM])
        b2 = sb("b2", [128, DIM])
        b2i = sb("b2i", [128, DIM], I32)
        b2q = sb("b2q", [128, DIM])
        b1 = sb("b1", [96, 128])
        b1i = sb("b1i", [96, 128], I32)
        b1f = sb("b1f", [96, 3, 128])
        b1_parts = sb("b1_parts", [96, 3, 128], BF16)
        b1_stack = sb("b1_stack", [96, 128], BF16)
        chunk_of_row = sb("chunk_of_row", [96, FC])
        chunk_ones = sb("chunk_ones", [96, FC, 128], BF16)
        w1 = sb("w1", [128, FC, DIM])
        w2 = sb("w2", [128, DC, FFN])
        w_i = [sb("w1_i", [128, 2048], I16), sb("w2_i", [128, 2048], I16)]
        w_q = [w_i[0][:, :].bitcast(BF16), w_i[1][:, :].bitcast(BF16)]
        w1T = sb("w1T", [128, DC, FC, 128], BF16)
        w2T = sb("w2T", [128, FC, DIM], BF16)
        s_act = sb("s_act", [128, 2])
        r_act = sb("r_act", [128, 2])
        wmax = sb("wmax", [128, 2])
        wmax_all = sb("wmax_all", [128, 2])
        r_wmax = sb("r_wmax", [128, 2])
        w_levels = sb("w_levels", [128, 2])
        w_scale = sb("w_scale", [128, 2])
        h_scale = sb("h_scale", [128, 2])
        r_h_scale = sb("r_h_scale", [128, 2])
        relu_scale = sb("relu_scale", [128, 1])
        n_ang = BATCH * 4
        x_all = sb("x_all", [128, BATCH, DIM])
        c_in = sb("c_in", [128, 2, CTX])
        pos_sb = sb("pos_sb", [128, BATCH, 2])
        ang = sb("ang", [128, BATCH, 2, 2])
        turns = sb("turns", [128, 2, n_ang], I32)
        red = sb("red", [128, 4, 2, n_ang])
        trig = sb("trig", [128, 2, n_ang])
        cos8 = sb("cos8", [128, BATCH, 4, 2])
        sin_neg = sb("sin_neg", [128, BATCH, 4])
        sin_pos = sb("sin_pos", [128, BATCH, 4])
        bn1 = sb("bn1", [128, 2, 6])
        mv1 = sb("mv1", [128, 2, 2])
        var1 = sb("var1", [128, 2, 1])
        rstd1 = sb("rstd1", [128, 2, 1])
        xn = sb("xn", [128, 2, DIM])
        xT = sb("xT", [128, 2, DIM + CTX])
        by_cos = sb("by_cos", [128, 2, 2 * DIM])
        by_sin = sb("by_sin", [128, 2, 2 * DIM])
        rot = sb("rot", [128, 2, 2 * DIM])
        q_rows = sb("q_rows", [128, 2, HEADS, 32])
        k_rows = sb("k_rows", [128, 2, HEADS, 32])
        q_comp = sb("q_comp", [128, 2, GROUPS, 128], F32R)
        k_stack = sb("k_stack", [128, 2, GROUPS, 128], F32R)
        q_diag = sb("q_diag", [128, 2, GROUPS, 512], F32R)
        v_comp = sb("v_comp", [128, 2, DIM])
        v_strip = sb("v_strip", [128, 2, HEADS, 32])
        mx = sb("mx", [128, 2, HEADS])
        mxT = sb("mxT", [16, 2, 2, 128], F32R)
        expo = sb("expo", [128, EXPO, 512])
        av = sb("av", [128, 2, 384])
        r_sum = sb("r_sum", [128, 2, HEADS])
        attn = sb("attn", [128, 2, DIM])
        attnT = sb("attnT", [128, 2, DIM])
        x_b = sb("x_b", [128, 2, DIM])
        x2 = sb("x2", [128, 2, DIM])
        bn2 = sb("bn2", [128, 2, 6])
        mv2 = sb("mv2", [128, 2, 2])
        var2 = sb("var2", [128, 2, 1])
        rstd2 = sb("rstd2", [128, 2, 1])
        xn2 = sb("xn2", [128, 2, DIM])
        xq_i = sb("xq_i", [128, 2, DIM], I16)
        xq = sb("xq", [128, 2, DIM], BF16)
        xqT = sb("xqT", [128, 2, DIM], BF16)
        h_i = sb("h_i", [128, 2, FC, 128], I16)
        hq = sb("hq", [128, 2, FC, 128], BF16)
        x2_b = sb("x2_b", [128, 2, DIM])
        y = sb("y", [128, 2, DIM])

        def bank(name):
            return stack.enter_context(nc.psum_tensor(name, [128, 512], F32))

        ps_max = [bank("ps_max0"), bank("ps_max1")]
        ps_exp = [bank("ps_exp0"), bank("ps_exp1")]
        ps_av = bank("ps_av")
        ps_misc = [bank(f"ps_misc{n}") for n in range(3)]

        loaded = sems("loaded", len(LOADS))
        c_loaded = sems("c_loaded")
        stored = sem("stored")
        early_loaded = sem("early_loaded")
        late_loaded = sem("late_loaded")
        diag_placed = [sems("diag_placed_lo"), sems("diag_placed_hi")]
        neg_placed = [sems("neg_placed_lo"), sems("neg_placed_hi")]
        id_ready = sem("id_ready")
        rope_step = sem("rope_step")
        ang_ready = sem("ang_ready")
        trig_ready = sem("trig_ready")
        wprep = sem("wprep")
        scales_ready = sem("scales_ready")
        bias_ready = sem("bias_ready")
        b1_cleared = sem("b1_cleared")
        wmax_ready = sem("wmax_ready")
        wmax_shared = sem("wmax_shared")
        wq_ready = sem("wq_ready")
        wT_in_psum = sem("wT_in_psum")
        wT_ready = sems("wT_ready")
        pads_ready = sem("pads_ready")
        zeros_ready = sem("zeros_ready")
        strips_ready = sem("strips_ready")
        ident_bf_ready = sem("ident_bf_ready")
        ln1_step = sem("ln1_step")
        var1_ready = sem("var1_ready")
        rstd1_ready = sem("rstd1_ready")
        xn_ready = sem("xn_ready")
        xT_in_psum = sem("xT_in_psum")
        xT_ready = sem("xT_ready")
        qk_in_psum = sem("qk_in_psum")
        rope_terms = sem("rope_terms")
        rot_ready = sem("rot_ready")
        hi_ready = sem("hi_ready")
        lo_ready = sem("lo_ready")
        v_in_psum = sem("v_in_psum")
        v_copied = sem("v_copied")
        v_ready = sem("v_ready")
        q_in_psum = sem("q_in_psum")
        q_ready = sem("q_ready")
        k_in_psum = sem("k_in_psum")
        k_ready = sem("k_ready")
        max_scores = sem("max_scores")
        max_done = sem("max_done")
        mx_in_psum = sem("mx_in_psum")
        mxT_ready = sem("mxT_ready")
        exp_scores = sem("exp_scores")
        exp_done = sem("exp_done")
        av_done = sem("av_done")
        av_copied = sem("av_copied")
        attn_in_psum = sem("attn_in_psum")
        r_sum_ready = sem("r_sum_ready")
        attn_ready = sem("attn_ready")
        attnT_in_psum = sem("attnT_in_psum")
        attnT_ready = sem("attnT_ready")
        wo_in_psum = sem("wo_in_psum")
        x_b_ready = sem("x_b_ready")
        x2_ready = sem("x2_ready")
        ln2_step = sem("ln2_step")
        var2_ready = sem("var2_ready")
        rstd2_ready = sem("rstd2_ready")
        xq_step = sem("xq_step")
        xq_ready = sem("xq_ready")
        xqT_in_psum = sem("xqT_in_psum")
        xqT_ready = sem("xqT_ready")
        h_in_psum = sem("h_in_psum")
        relu_done = sem("relu_done")
        hq_ready = sem("hq_ready")
        y_in_psum = sem("y_in_psum")
        x2_b_ready = sem("x2_b_ready")
        y_ready = sem("y_ready")

        block = stack.enter_context(nc.Block())

        def copy_wT(eng, n):
            src = ps_exp[n % 2][:, 0:256].bitcast(BF16).rearrange("p (f c) -> p f c", f=4)
            which, c, quarter = n // 4, n // 2 % 2, n % 2
            fs = slice(4 * quarter, 4 * quarter + 4)
            dst = w1T[:, c, fs, :] if which == 0 else w2T[:, fs, 128 * c:128 * c + 128]
            return eng.tensor_copy(dst, src) if eng is nc.vector else eng.copy(dst, src)

        def copy_weights(eng, bank_n):
            for n in range(bank_n, 8, 2):
                eng.wait_ge(wT_in_psum, n + 1)
                copy_wT(eng, n).then_inc(wT_ready[bank_n], 1)

        out_pairs = out_d.rearrange("(k two) t d -> k t two d", two=2)

        def wait_loaded(eng, st, stage):
            if not st.looped:
                b = st.s - stage
                for n, (lo, hi) in enumerate(LOADS):
                    if lo == b or (st.s == LOOP_FROM - 1 and lo > b):
                        eng.wait_ge(loaded[n], 16)

        def all_rows(ap):
            return bcast(ap, 0, 128)

        @block.sync
        def _(sp):
            def load(n):
                lo, hi = LOADS[n]
                sp.dma_start(x_all[:, lo:hi, :], x[lo:hi].rearrange("b t d -> t b d")).then_inc(loaded[n], 16)

            def load_context(st):
                r, b = st.ring(S_NORM), st.batch(S_NORM)
                st.wait(sp, xT_in_psum, S_NORM, 1, -1)
                sp.dma_start(c_in[:, r, :], ctx_in[b]).then_inc(c_loaded[r], 16)

            def place_queries(st, half):
                r = st.ring(S_STACK)
                gs = slice(4 * half, 4 * half + 4)
                st.wait(sp, q_ready, S_STACK, 2, half + 1)
                st.wait(sp, exp_scores, S_STACK, GROUPS, 4 * half + 4 - 2 * GROUPS)
                if not st.looped and half == 0 and st.s < S_STACK + 2:
                    sp.wait_ge(zeros_ready, r + 1)
                for j in range(4):
                    rows, cols = slice(32 * j, 32 * j + 32), slice(128 * j, 128 * j + 128)
                    sp.dma_start(q_diag[rows, r, gs, cols].bitcast(F32), q_comp[rows, r, gs, :].bitcast(F32))\
                      .then_inc(diag_placed[half][r], 16)

            def place_maxima(st, half, stage):
                r = st.ring(stage)
                st.wait(sp, mxT_ready, stage, 2, half + 1)
                dst = q_diag[NEG_ROW:NEG_ROW + 1, r, 4 * half:4 * half + 4, :].rearrange("o g (j t) -> o (g j) t", j=4)
                sp.dma_start(dst.bitcast(F32), mxT[:, r, half, :].bitcast(F32)).then_inc(neg_placed[half][r], 16)

            def store(st):
                st.wait(sp, y_ready, S_FFN, 1, 1)
                pair = st.value(1, (st.s - S_FFN) // 2)
                sp.dma_start(out_pairs[pair], y[:, :, :]).then_inc(stored, 16)

            def body(st):
                if st.has(S_NORM) and st.s > 0:
                    load_context(st)
                if st.has(S_ATT):
                    place_maxima(st, 1, S_ATT)
                if st.has(S_STACK):
                    place_queries(st, 0)
                if st.has(S_MAX):
                    place_maxima(st, 0, S_MAX)
                if st.has(S_STACK):
                    place_queries(st, 1)
                if st.has(S_FFN) and st.ring(S_FFN) == 1:
                    store(st)

            load(0)
            load_context(Step(0, 0, False))
            for c in range(DC):
                sp.dma_start(wq[:, c, :], wq_d[128 * c:128 * c + 128, :]).then_inc(early_loaded, 16)
            sp.dma_start(wkv[:, :], wkv_d).then_inc(early_loaded, 16)
            load(1)
            sp.dma_start(w1[:, :, :], w1_d.rearrange("(c p) d -> p c d", p=128)).then_inc(late_loaded, 16)
            sp.dma_start(w2[:, :, :], w2_d.rearrange("(c p) f -> p c f", p=128)).then_inc(late_loaded, 16)
            load(2)
            late = [
                (wout[:, :, :], wout_d.rearrange("(c p) d -> p c d", p=128)),
                (bout[:, :], all_rows(bout_d)),
                (b2[:, :], all_rows(b2_d)),
                (s_act[:, 0:1], all_rows(s1_d)),
                (s_act[:, 1:2], all_rows(s2_d)),
            ]
            sp.wait_ge(b1_cleared, 1)
            late += [(b1[32 * n:32 * n + FC, :], b1_d.rearrange("(c p) -> c p", p=128)) for n in range(3)]
            for dst, src in late:
                sp.dma_start(dst, src, allow_slow_non_contiguous=True).then_inc(late_loaded, 16)
            load(3)
            load(4)

            def hold(st):
                for half in range(2):
                    st.hold(sp, S_STACK, GROUPS, 4 * half + 4 - 2 * GROUPS)

            run_steps(sp, body, hold)
            sp.wait_ge(stored, 16 * BATCH // 2)

        LATE = 16 * 10
        EARLY = 16 * 3
        POS = sem("pos_loaded")

        @block.gpsimd
        def _(pool):
            pool.memset(b1[:, :], 0.0).then_inc(b1_cleared, 1)
            pool.memset(ident[:, :], 0.0).then_inc(id_ready, 1)
            pool.wait_ge(id_ready, 1)
            pool.affine_select(out=ident[:, :], in_=ident[:, :], compare_op=ALU.not_equal, fill=1.0,
                               base=0, pattern=[[-1, 128]], channel_multiplier=1).then_inc(id_ready, 1)
            pool.memset(zeros[:, :], 0.0).then_inc(id_ready, 1)
            pool.memset(minus_half[:, :], -0.5).then_inc(id_ready, 1)
            pool.wait_ge(id_ready, 4)
            pool.memset(q_rows[:, :, :, :], 0.0).then_inc(pads_ready, 1)
            pool.memset(k_rows[:, :, :, :], 0.0).then_inc(pads_ready, 1)
            pool.wait_ge(pads_ready, 2)
            pool.memset(k_rows[:, :, NEG_ROW // 32::4, NEG_ROW % 32:NEG_ROW % 32 + 1], -1.0).then_inc(pads_ready, 1)

            def clear_diagonal(r):
                pool.memset(q_diag[:, r, :, :].bitcast(I32), 0).then_inc(zeros_ready, 1)

            def fill_strips():
                pool.memset(v_strip[:, :, :, :], 0.0).then_inc(strips_ready, 1)
                pool.wait_ge(strips_ready, 1)
                for s in range(VREG):
                    for g in range(s, GROUPS, VREG):
                        ins = pool.memset(v_strip[:, :, 4 * g:4 * g + 4, 9 * s + HD:9 * s + HD + 1], 1.0)
                ins.then_inc(strips_ready, 1)

            def norm(st):
                r = st.ring(S_NORM)
                st.wait(pool, var1_ready, S_NORM, 1, 1)
                st.wait(pool, xn_ready, S_NORM, 1, -1)
                pool.tensor_tensor(rstd1[:, r, :], var1[:, r, :], minus_half[:, :], ALU.pow).then_inc(rstd1_ready, 1)

            def rotate(st):
                r = st.ring(S_PROJ)
                st.wait(pool, rope_terms, S_PROJ, 3, 3)
                st.wait(pool, hi_ready, S_PROJ, 2, -2)
                st.wait(pool, lo_ready, S_PROJ, 2, -2)
                pool.tensor_tensor(rot[:, r, :], by_cos[:, r, :], by_sin[:, r, :], ALU.add).then_inc(rot_ready, 1)

            def split_low(st, n):
                r = st.ring(S_PROJ)
                rows, at = (q_rows, k_rows)[n], (16, 8)[n]
                st.wait(pool, hi_ready, S_PROJ, 2, n + 1)
                src = rot[:, r, n * DIM:(n + 1) * DIM].rearrange("p (h d) -> p h d", d=HD)
                pool.tensor_tensor(rows[:, r, :, at:at + HD], src, rows[:, r, :, 0:HD], ALU.subtract)\
                    .then_inc(lo_ready, 1)

            def place_values(st):
                r = st.ring(S_MAX)
                st.wait(pool, v_copied, S_MAX, 1, 1)
                st.wait(pool, av_done, S_MAX, GROUPS, -GROUPS)
                if not st.looped and st.s == S_MAX:
                    pool.wait_ge(strips_ready, 2)
                for region in range(3):
                    n = min(VREG, GROUPS - VREG * region)
                    h = 4 * VREG * region
                    strips = v_strip[:, r, h:h + 4 * n, :].rearrange("p (s i) c -> p s i c", s=n)
                    for s in range(n):
                        vals = v_comp[:, r, (h + 4 * s) * HD:(h + 4 * s + 4) * HD].rearrange("p (i d) -> p i d", d=HD)
                        nothing = bcast(zeros[:, 0:HD], 1, 4)
                        ins = pool.tensor_tensor(strips[:, s, :, 9 * s:9 * s + HD], vals, nothing, ALU.add)
                ins.then_inc(v_ready, 1)

            def residual_bias(st):
                r = st.ring(S_ATT)
                wait_loaded(pool, st, S_ATT)
                if not st.looped and st.s == S_ATT:
                    pool.wait_ge(late_loaded, LATE)
                st.wait(pool, x2_ready, S_ATT, 1, -1)
                pool.tensor_tensor(x_b[:, r, :], x_all[:, st.batch(S_ATT), :], bout[:, :], ALU.add).then_inc(x_b_ready, 1)

            def norm2(st):
                r = st.ring(S_OUT)
                st.wait(pool, var2_ready, S_OUT, 1, 1)
                st.wait(pool, xq_ready, S_OUT, 1, -1)
                pool.tensor_tensor(rstd2[:, r, :], var2[:, r, :], minus_half[:, :], ALU.pow).then_inc(rstd2_ready, 1)

            def output_bias(st):
                r = st.ring(S_OUT)
                st.wait(pool, x2_ready, S_OUT, 1, 1)
                st.wait(pool, y_ready, S_OUT, 1, -1)
                pool.tensor_tensor(x2_b[:, r, :], x2[:, r, :], b2q[:, :], ALU.add).then_inc(x2_b_ready, 1)

            def body(st):
                if not st.looped and st.s == 1:
                    clear_diagonal(1)
                    fill_strips()
                if not st.looped and st.s == 2:
                    pool.wait_ge(wmax_ready, 2)
                    pool.partition_all_reduce(wmax_all[:, :], wmax[:, :], 128, bass.bass_isa.ReduceOp.max)\
                        .then_inc(wmax_shared, 1)
                if not st.looped and st.s == S_OUT:
                    pool.wait_ge(bias_ready, 2)
                if st.has(S_MAX):
                    place_values(st)
                if st.has(S_ATT):
                    residual_bias(st)
                if st.has(S_PROJ):
                    rotate(st)
                    split_low(st, 0)
                if not st.looped and st.s == 0:
                    clear_diagonal(0)
                if st.has(S_NORM):
                    norm(st)
                if st.has(S_PROJ):
                    split_low(st, 1)
                if st.has(S_OUT):
                    norm2(st)
                    output_bias(st)

            run_steps(pool, body)

        @block.scalar
        def _(act):
            act.dma_start(pos_sb[:, :, :], pos.rearrange("b t p -> t b p")).then_inc(POS, 16)
            act.wait_ge(id_ready, 2)
            act.copy(ident_bf[:, :], ident[:, :]).then_inc(ident_bf_ready, 1)
            act.wait_ge(ang_ready, 1)
            act.activation(trig[:, :, :], red[:, 3, :, :], ACT.Sin).then_inc(trig_ready, 1)

            def copy_xT(st):
                r = st.ring(S_PROJ)
                st.wait(act, xT_in_psum, S_PROJ, 1, 1)
                st.wait(act, v_in_psum, S_PROJ, 1, -1)
                act.copy(xT[:, r, :], ps_misc[PIECE_BANK[XT]][:, 0:DIM + CTX]).then_inc(xT_ready, 1)

            def split_high(st, n):
                r = st.ring(S_PROJ)
                st.wait(act, rot_ready, S_PROJ, 1, 1)
                if not st.looped and st.s == S_PROJ:
                    act.wait_ge(pads_ready, 3)
                st.wait(act, (q_in_psum, k_in_psum)[n], S_PROJ, 2, -2)
                src = bcast(rot[:, r, n * DIM:(n + 1) * DIM].rearrange("p (h d) -> p h d", d=HD), 2, 2)
                rows = (q_rows, k_rows)[n][:, r, :, :].bitcast(F32R).rearrange("p h (c d) -> p h c d", d=HD)
                act.copy(rows[:, :, 0:2, :] if n == 0 else rows[:, :, 0:3:2, :], src).then_inc(hi_ready, 1)

            def copy_v(st):
                r = st.ring(S_PROJ)
                st.wait(act, v_in_psum, S_PROJ, 1, 1)
                st.wait(act, v_ready, S_PROJ, 1, -1)
                act.copy(v_comp[:, r, :], ps_misc[PIECE_BANK[VV]][:, 0:DIM]).then_inc(v_copied, 1)

            def copy_keys(st, half):
                r = st.ring(S_STACK)
                st.wait(act, k_in_psum, S_STACK, 2, half + 1)
                st.wait(act, exp_scores, S_STACK, GROUPS, 4 * half + 4 - 2 * GROUPS)
                act.copy(k_stack[:, r, 4 * half:4 * half + 4, :],
                         ps_misc[PIECE_BANK[(SK0, SK1)[half]]][:, :].rearrange("p (g t) -> p g t", g=4)).then_inc(k_ready, 1)

            def exponentials(st, g):
                st.wait(act, exp_scores, S_ATT, GROUPS, g + 1)
                st.wait(act, av_done, S_ATT, GROUPS, g + 1 - EXPO)
                act.activation(expo[:, g % EXPO, :], ps_exp[g % 2][:, :], ACT.Exp, scale=SCALE).then_inc(exp_done, 1)

            def copy_av(st):
                r = st.ring(S_OUT)
                st.wait(act, av_done, S_OUT, GROUPS, GROUPS)
                st.wait(act, attn_in_psum, S_OUT, 1, -1)
                act.copy(av[:, r, :], ps_av[:, 0:384]).then_inc(av_copied, 1)

            def copy_attnT(st):
                r = st.ring(S_OUT)
                st.wait(act, attnT_in_psum, S_OUT, 1, 1)
                st.wait(act, wo_in_psum, S_OUT, 1, -1)
                act.copy(attnT[:, r, :], ps_misc[PIECE_BANK[AT2]][:, 0:DIM]).then_inc(attnT_ready, 1)

            def copy_xqT(st):
                r = st.ring(S_FFN)
                st.wait(act, xqT_in_psum, S_FFN, 1, 1)
                st.wait(act, h_in_psum, S_FFN, 2, -2)
                act.copy(xqT[:, r, :], ps_misc[PIECE_BANK[XQ]][:, 0:DIM // 2].bitcast(BF16)).then_inc(xqT_ready, 1)

            def relu(st, half):
                r = st.ring(S_FFN)
                st.wait(act, h_in_psum, S_FFN, 2, half + 1)
                st.wait(act, hq_ready, S_FFN, 2, half - 3)
                if not st.looped and st.s == S_FFN and half == 0:
                    act.wait_ge(scales_ready, 1)
                act.activation(h_i[:, r, 4 * half:4 * half + 4, :].rearrange("p f t -> p (f t)"),
                               ps_misc[PIECE_BANK[(H0, H1)[half]]][:, :], ACT.Relu, scale=relu_scale[:, :])\
                   .then_inc(relu_done, 1)

            def body(st):
                for g in range(GROUPS):
                    if g == LAG and st.has(S_OUT):
                        copy_av(st)
                    if st.has(S_ATT):
                        exponentials(st, g)
                    if g == 0 and st.has(S_PROJ):
                        copy_xT(st)
                    if g == 2 and st.has(S_FFN):
                        copy_xqT(st)
                    if g == 3 and st.has(S_FFN):
                        relu(st, 0)
                    if g == 4 and st.has(S_PROJ):
                        split_high(st, 0)
                    if g == 4 and st.has(S_FFN):
                        relu(st, 1)
                    if g == 5 and st.has(S_OUT):
                        copy_attnT(st)
                    if g == 5 and st.has(S_PROJ):
                        copy_v(st)
                    if g == 6 and st.has(S_PROJ):
                        split_high(st, 1)
                    if g == 6 and st.has(S_STACK):
                        copy_keys(st, 0)
                    if g == 7 and st.has(S_STACK):
                        copy_keys(st, 1)
                if not st.looped and st.s == S_ATT - 1:
                    copy_weights(act, 1)

            run_steps(act, body)

        @block.vector
        def _(dve):
            steps = [0]

            def link(ins, chain):
                steps[0] += 1
                ins.then_inc(chain, 1)
                dve.wait_ge(chain, steps[0])

            def rope_tables():
                dve.wait_ge(POS, 16)
                for f, freq in enumerate((1.0, ROPE_FREQ)):
                    link(dve.tensor_scalar(ang[:, :, :, f], pos_sb[:, :, :], freq, None, ALU.mult), rope_step)
                angles = ang[:, :, :, :].rearrange("p b a f -> p (b a f)")
                for n in range(2):
                    link(dve.tensor_scalar(turns[:, n, :], angles, 1.0 / (2 * np.pi), 0.25 * n, ALU.mult, ALU.add), rope_step)
                    link(dve.tensor_copy(red[:, 0, n, :], turns[:, n, :]), rope_step)
                    link(dve.scalar_tensor_tensor(out=red[:, 1, n, :], in0=red[:, 0, n, :], scalar=-TWO_PI_HI, in1=angles,
                                                  op0=ALU.mult, op1=ALU.add), rope_step)
                    link(dve.scalar_tensor_tensor(out=red[:, 2, n, :], in0=red[:, 0, n, :], scalar=-TWO_PI_MID,
                                                  in1=red[:, 1, n, :], op0=ALU.mult, op1=ALU.add), rope_step)
                    link(dve.scalar_tensor_tensor(out=red[:, 1, n, :], in0=red[:, 0, n, :], scalar=-TWO_PI_LO,
                                                  in1=red[:, 2, n, :], op0=ALU.mult, op1=ALU.add), rope_step)
                    link(dve.tensor_scalar(red[:, 2, n, :], red[:, 1, n, :], 0.5 * np.pi * n, SIN_LIMIT, ALU.add, ALU.min),
                         rope_step)
                    link(dve.tensor_scalar(red[:, 3, n, :], red[:, 2, n, :], -SIN_LIMIT, None, ALU.max), rope_step)
                dve.wait_ge(rope_step, steps[0])
                dve.tensor_copy(red[:, 0, 0, 0:1], red[:, 3, 0, 0:1]).then_inc(ang_ready, 1)
                dve.wait_ge(trig_ready, 1)
                sine = trig[:, 0, :].rearrange("p (b f) -> p b f", b=BATCH)
                cosine = trig[:, 1, :].rearrange("p (b f) -> p b f", b=BATCH)
                dve.tensor_copy(cos8[:, :, :, 0], cosine)
                dve.tensor_copy(cos8[:, :, :, 1], cosine)
                dve.tensor_scalar(sin_neg[:, :, :], sine, -1.0, None, ALU.mult)
                link(dve.tensor_copy(sin_pos[:, :, :], sine), rope_step)

            w_flat = [w1[:, :, :].rearrange("p c d -> p (c d)"), w2[:, :, :].rearrange("p c f -> p (c f)")]

            def weight_maxima():
                dve.wait_ge(late_loaded, LATE)
                for n in range(2):
                    dve.tensor_reduce(out=wmax[:, n:n + 1], in_=w_flat[n], axis=AX.X, op=ALU.max,
                                      apply_absolute_value=True).then_inc(wmax_ready, 1)

            def quantise_weights(n):
                if n == 0:
                    steps[0] = 0
                    dve.wait_ge(wmax_shared, 1)
                    link(dve.reciprocal(r_wmax[:, :], wmax_all[:, :]), wprep)
                    link(dve.tensor_scalar(w_levels[:, :], r_wmax[:, :], QMAX, None, ALU.mult), wprep)
                link(dve.tensor_scalar(w_i[n][:, :], w_flat[n], w_levels[:, n:n + 1], None, ALU.mult), wprep)
                dve.tensor_scalar(w_q[n][:, :], w_i[n][:, :], QMIN, QMAX, ALU.max, ALU.min).then_inc(wq_ready, 1)

            def prepare_scales():
                link(dve.reciprocal(r_act[:, :], s_act[:, :]), wprep)
                link(dve.tensor_scalar(w_scale[:, :], wmax_all[:, :], 1.0 / QMAX, None, ALU.mult), wprep)
                link(dve.tensor_tensor(h_scale[:, :], w_scale[:, :], s_act[:, :], ALU.mult), wprep)
                link(dve.reciprocal(r_h_scale[:, :], h_scale[:, :]), wprep)
                dve.tensor_tensor(relu_scale[:, :], h_scale[:, 0:1], r_act[:, 1:2], ALU.mult).then_inc(scales_ready, 1)

            def prepare_biases():
                link(dve.tensor_scalar(b2i[:, :], b2[:, :], r_h_scale[:, 1:2], None, ALU.mult), wprep)
                dve.tensor_scalar(b2q[:, :], b2i[:, :], h_scale[:, 1:2], None, ALU.mult).then_inc(bias_ready, 1)
                link(dve.tensor_scalar(b1i[:, :], b1[:, :], r_h_scale[0:96, 0:1], None, ALU.mult), wprep)
                link(dve.tensor_copy(b1f[:, 0, :], b1i[:, :]), wprep)
                for n in range(3):
                    link(dve.tensor_copy(b1_parts[:, n, :], b1f[:, n, :]), wprep)
                    if n < 2:
                        link(dve.tensor_tensor(b1f[:, n + 1, :], b1f[:, n, :], b1_parts[:, n, :], ALU.subtract), wprep)
                for n in range(3):
                    rows = slice(32 * n, 32 * n + 32)
                    dve.tensor_copy(b1_stack[rows, :], b1_parts[rows, n, :])
                link(dve.tensor_reduce(out=chunk_of_row[:, :],
                                       in_=ident[0:96, 0:96].rearrange("p (n f) -> p f n", n=3)[:, 0:FC, :],
                                       axis=AX.X, op=ALU.max), wprep)
                dve.tensor_copy(chunk_ones[:, :, :], bcast(chunk_of_row[:, :], 2, 128)).then_inc(bias_ready, 1)

            def norm1_stats(st):
                r = st.ring(S_NORM)
                wait_loaded(dve, st, S_NORM)
                dve.bn_stats(bn1[:, r, :], x_all[:, st.batch(S_NORM), :]).then_inc(ln1_step, 1)

            def norm1_moments(st):
                r = st.ring(S_NORM)
                dve.bn_aggr(mv1[:, r, :], bn1[:, r, :]).then_inc(ln1_step, 1)
                st.wait(dve, ln1_step, S_NORM, 2, 2)
                st.wait(dve, rstd1_ready, S_NORM, 1, -1)
                dve.tensor_scalar(var1[:, r, :], mv1[:, r, 1:2], EPS, None, ALU.add).then_inc(var1_ready, 1)

            def norm1(st):
                r = st.ring(S_NORM)
                st.wait(dve, rstd1_ready, S_NORM, 1, 1)
                st.wait(dve, xT_in_psum, S_NORM, 1, -1)
                dve.tensor_scalar(xn[:, r, :], x_all[:, st.batch(S_NORM), :], mv1[:, r, 0:1], rstd1[:, r, :],
                                  ALU.subtract, ALU.mult).then_inc(xn_ready, 1)

            def rope(st):
                r, b = st.ring(S_PROJ), st.batch(S_PROJ)
                st.wait(dve, qk_in_psum, S_PROJ, 1, 1)
                st.wait(dve, rot_ready, S_PROJ, 1, -1)
                ps = ps_misc[PIECE_BANK[QK]][:, :]
                cos_b = bcast(cos8[:, b, :, :].rearrange("p f c -> p (f c)"), 1, 2 * HEADS)
                dve.tensor_tensor(by_cos[:, r, :].rearrange("p (h d) -> p h d", d=HD),
                                  ps.rearrange("p (h d) -> p h d", d=HD), cos_b, ALU.mult).then_inc(rope_terms, 1)
                pairs_in = ps.rearrange("p (h f c) -> p h f c", f=4, c=2)
                pairs_out = by_sin[:, r, :].rearrange("p (h f c) -> p h f c", f=4, c=2)
                for c, s in enumerate((sin_neg, sin_pos)):
                    dve.tensor_tensor(pairs_out[:, :, :, c], pairs_in[:, :, :, 1 - c],
                                      bcast(s[:, b, :], 1, 2 * HEADS), ALU.mult).then_inc(rope_terms, 1)

            def copy_queries(st, half):
                r = st.ring(S_STACK)
                st.wait(dve, q_in_psum, S_STACK, 2, half + 1)
                st.wait_dma(dve, diag_placed[half], S_STACK, 64, back=1)
                dve.tensor_copy(q_comp[:, r, 4 * half:4 * half + 4, :],
                                ps_misc[PIECE_BANK[(SQ0, SQ1)[half]]][:, :].rearrange("p (g t) -> p g t", g=4))\
                   .then_inc(q_ready, 1)

            def maxima(st, g):
                r = st.ring(S_MAX)
                st.wait(dve, max_scores, S_MAX, GROUPS, g + 1)
                if g == 0:
                    st.wait(dve, mx_in_psum, S_MAX, 2, -2)
                dve.tensor_reduce(out=mx[:, r, 4 * g:4 * g + 4],
                                  in_=ps_max[g % 2][:, :].rearrange("p (h k) -> p h k", h=4),
                                  axis=AX.X, op=ALU.max).then_inc(max_done, 1)

            def copy_maxima(st, half, stage):
                r = st.ring(stage)
                st.wait(dve, mx_in_psum, stage, 2, half + 1)
                st.wait_dma(dve, neg_placed[half], stage, 16, back=1)
                dve.tensor_copy(mxT[:, r, half, :], ps_misc[PIECE_BANK[(MX0, MX1)[half]]][0:16, 0:128]).then_inc(mxT_ready, 1)

            def normalise(st):
                r = st.ring(S_OUT)
                st.wait(dve, attn_in_psum, S_OUT, 1, 1)
                st.wait(dve, attn_ready, S_OUT, 1, -1)
                st.wait(dve, attnT_in_psum, S_OUT, 1, -1)
                for region in range(3):
                    n = min(VREG, GROUPS - VREG * region)
                    cols = ps_misc[PIECE_BANK[AT1]][:, 128 * region:128 * region + 128].rearrange("p (i c) -> p i c", i=4)
                    sums = cols[:, :, 0:9 * n].rearrange("p i (s d) -> p s i d", d=9)[:, :, :, HD:HD + 1]
                    h = 4 * VREG * region
                    ins = dve.reciprocal(r_sum[:, r, h:h + 4 * n].rearrange("p (s i d) -> p s i d", s=n, d=1), sums)
                ins.then_inc(r_sum_ready, 1)
                st.wait(dve, r_sum_ready, S_OUT, 1, 1)
                for region in range(3):
                    n = min(VREG, GROUPS - VREG * region)
                    cols = ps_misc[PIECE_BANK[AT1]][:, 128 * region:128 * region + 128].rearrange("p (i c) -> p i c", i=4)
                    vals = cols[:, :, 0:9 * n].rearrange("p i (s d) -> p s i d", d=9)[:, :, :, 0:HD]
                    h = 4 * VREG * region
                    scale = bcast(r_sum[:, r, h:h + 4 * n].rearrange("p (s i) -> p s i", s=n), 3, HD)
                    dst = attn[:, r, h * HD:(h + 4 * n) * HD].rearrange("p (s i d) -> p s i d", s=n, d=HD)
                    ins = dve.tensor_tensor(dst, vals, scale, ALU.mult)
                ins.then_inc(attn_ready, 1)

            def residual(st):
                r = st.ring(S_OUT)
                st.wait(dve, wo_in_psum, S_OUT, 1, 1)
                st.wait(dve, x_b_ready, S_OUT, 1, 1)
                st.wait(dve, x2_b_ready, S_OUT, 1, -1)
                dve.tensor_tensor(x2[:, r, :], ps_misc[PIECE_BANK[WO]][:, 0:DIM], x_b[:, r, :], ALU.add).then_inc(x2_ready, 1)
                st.wait(dve, x2_ready, S_OUT, 1, 1)
                dve.bn_stats(bn2[:, r, :], x2[:, r, :]).then_inc(ln2_step, 1)

            def norm2_moments(st):
                r = st.ring(S_OUT)
                dve.bn_aggr(mv2[:, r, :], bn2[:, r, :]).then_inc(ln2_step, 1)
                st.wait(dve, ln2_step, S_OUT, 2, 2)
                st.wait(dve, rstd2_ready, S_OUT, 1, -1)
                dve.tensor_scalar(var2[:, r, :], mv2[:, r, 1:2], EPS, None, ALU.add).then_inc(var2_ready, 1)

            def quantise_x(st):
                r = st.ring(S_FFN)
                st.wait(dve, rstd2_ready, S_FFN, 1, 1)
                dve.tensor_scalar(xn2[:, r, :], x2[:, r, :], mv2[:, r, 0:1], rstd2[:, r, :],
                                  ALU.subtract, ALU.mult).then_inc(xq_step, 1)
                st.wait(dve, xq_step, S_FFN, 2, 1)
                dve.tensor_scalar(xq_i[:, r, :], xn2[:, r, :], r_act[:, 0:1], None, ALU.mult).then_inc(xq_step, 1)
                st.wait(dve, xq_step, S_FFN, 2, 2)
                st.wait(dve, xqT_in_psum, S_FFN, 1, -1)
                dve.tensor_scalar(xq[:, r, :], xq_i[:, r, :], QMIN, QMAX, ALU.max, ALU.min).then_inc(xq_ready, 1)

            def clip_h(st, half):
                r = st.ring(S_FFN)
                fs = slice(4 * half, 4 * half + 4)
                st.wait(dve, relu_done, S_FFN, 2, half + 1)
                st.wait(dve, y_in_psum, S_FFN, 1, -1)
                dve.tensor_scalar(hq[:, r, fs, :], h_i[:, r, fs, :], 0.0, HMAX, ALU.max, ALU.min).then_inc(hq_ready, 1)

            def output(st):
                r = st.ring(S_FFN)
                st.wait(dve, y_in_psum, S_FFN, 1, 1)
                st.wait(dve, x2_b_ready, S_FFN, 1, 1)
                st.wait_dma(dve, [stored, stored], S_FFN, 16, back=1)
                dve.scalar_tensor_tensor(out=y[:, r, :], in0=ps_misc[PIECE_BANK[YY]][:, 0:DIM], scalar=h_scale[:, 1:2],
                                         in1=x2_b[:, r, :], op0=ALU.mult, op1=ALU.add).then_inc(y_ready, 1)

            def body(st):
                for g in range(GROUPS):
                    if g == 5 and st.has(S_NORM):
                        st.wait(dve, ln1_step, S_NORM, 2, 1)
                    if g == 7 and st.has(S_OUT):
                        st.wait(dve, ln2_step, S_OUT, 2, 1)
                    if st.has(S_MAX):
                        maxima(st, g)
                    if g == 0 and st.has(S_STACK):
                        copy_queries(st, 0)
                    if g == 0 and st.has(S_FFN):
                        quantise_x(st)
                    if g == 1 and st.has(S_ATT):
                        copy_maxima(st, 1, S_ATT)
                    if g == 1 and st.has(S_PROJ):
                        rope(st)
                    if g == 2 and st.has(S_STACK):
                        copy_queries(st, 1)
                    if g == 3 and st.has(S_OUT):
                        normalise(st)
                    if g == 4 and st.has(S_NORM):
                        norm1_stats(st)
                    if g == 5 and st.has(S_NORM):
                        norm1_moments(st)
                    if g == 5 and not st.looped and st.s == 0:
                        rope_tables()
                    if g == 4 and st.has(S_MAX):
                        copy_maxima(st, 0, S_MAX)
                    if g == 5 and st.has(S_FFN):
                        clip_h(st, 0)
                    if g == 6 and st.has(S_NORM):
                        norm1(st)
                    if g == 6 and st.has(S_FFN):
                        clip_h(st, 1)
                    if g == 6 and st.has(S_OUT):
                        residual(st)
                    if g == 7 and st.has(S_OUT):
                        norm2_moments(st)
                    if g == 7 and st.has(S_FFN):
                        output(st)
                if not st.looped and st.s == 1:
                    weight_maxima()
                if not st.looped and st.s == 2:
                    quantise_weights(0)
                if not st.looped and st.s == 3:
                    quantise_weights(1)
                    copy_weights(dve, 0)
                    prepare_scales()
                if not st.looped and st.s == 4:
                    prepare_biases()

            run_steps(dve, body)

        @block.tensor
        def _(pe):
            def mm(out, lhsT, rhs, start=True, stop=True, **kw):
                return pe.matmul(out, lhsT, rhs, start=start, stop=stop, skip_group_check=True, **kw)

            def transpose(out, in_, idn):
                return mm(out, in_, idn, is_transpose=True)

            emptied = {
                XT: (xT_ready, S_PROJ, 1, 1), SQ0: (q_ready, S_STACK, 2, 1), MX1: (mxT_ready, S_ATT, 2, 2),
                QK: (rope_terms, S_PROJ, 3, 3), AT1: (attn_ready, S_OUT, 1, 1), XQ: (xqT_ready, S_FFN, 1, 1),
                SQ1: (q_ready, S_STACK, 2, 2), H0: (relu_done, S_FFN, 2, 1), AT2: (attnT_ready, S_OUT, 1, 1),
                H1: (relu_done, S_FFN, 2, 2), WO: (x2_ready, S_OUT, 1, 1), MX0: (mxT_ready, S_MAX, 2, 1),
                VV: (v_copied, S_PROJ, 1, 1), SK0: (k_ready, S_STACK, 2, 1), YY: (y_ready, S_FFN, 1, 1),
                SK1: (k_ready, S_STACK, 2, 2),
            }

            def claim(st, piece):
                bank_n = PIECE_BANK[piece]
                for back in range(1, 2 * PIECES):
                    p = (piece - back) % PIECES
                    prev = Step(st.it, st.s + (piece - back) // PIECES, st.looped, st.held)
                    s_, stage, per, k = emptied[p]
                    if PIECE_BANK[p] == bank_n and prev.has(stage):
                        prev.wait(pe, s_, stage, per, k)
                        break
                return ps_misc[bank_n]

            def transpose_x(st):
                ps, r = claim(st, XT), st.ring(S_PROJ)
                st.wait(pe, xn_ready, S_PROJ, 1, 1)
                st.wait_dma(pe, c_loaded, S_PROJ, 16)
                for c in range(DC):
                    transpose(ps[:, 128 * c:128 * c + 128], xn[:, r, 128 * c:128 * c + 128], ident[:, :])
                transpose(ps[:, DIM:DIM + CTX], c_in[:, r, :], ident[:, :]).then_inc(xT_in_psum, 1)

            def project_qk(st):
                ps, r = claim(st, QK), st.ring(S_PROJ)
                st.wait(pe, xT_ready, S_PROJ, 1, 1)
                for c in range(DC):
                    mm(ps[:, 0:DIM], xT[:, r, 128 * c:128 * c + 128], wq[:, c, :], c == 0, c == DC - 1)
                mm(ps[:, DIM:2 * DIM], xT[:, r, DIM:DIM + CTX], wkv[:, 0:DIM]).then_inc(qk_in_psum, 1)

            def project_v(st):
                ps, r = claim(st, VV), st.ring(S_PROJ)
                mm(ps[:, 0:DIM], xT[:, r, DIM:DIM + CTX], wkv[:, DIM:2 * DIM]).then_inc(v_in_psum, 1)

            def transpose_rows(st, piece, rows, in_psum, ready, half):
                ps, r = claim(st, piece), st.ring(S_STACK)
                st.wait(pe, lo_ready, S_STACK, 2, ready)
                for g in range(4):
                    h = 4 * (4 * half + g)
                    ins = transpose(ps[:, 128 * g:128 * g + 128], rows[:, r, h:h + 4, :].rearrange("p h c -> p (h c)"),
                                    ident[:, :])
                ins.then_inc(in_psum, 1)

            def scores_for_max(st, g):
                r = st.ring(S_MAX)
                if g % 4 == 0:
                    st.wait_dma(pe, diag_placed[g // 4], S_MAX, 64)
                    st.wait(pe, k_ready, S_MAX, 2, g // 4 + 1)
                st.wait(pe, max_done, S_MAX, GROUPS, g - 1)
                keys = k_stack[:, r, g, :].bitcast(BF16).rearrange("p (t w) -> p t w", w=2)[:, :, 1]
                queries = q_diag[:, r, g, :].bitcast(BF16).rearrange("p (t w) -> p t w", w=2)[:, :, 1]
                for i in range(4):
                    rows = slice(0, 96 if i < 3 else 128)
                    ins = mm(ps_max[g % 2][:, 128 * i:128 * i + 128], queries[rows, 128 * i:128 * i + 128], keys[rows])
                ins.then_inc(max_scores, 1)

            def transpose_maxima(st, half, stage, piece):
                ps, r = claim(st, piece), st.ring(stage)
                st.wait(pe, max_done, stage, GROUPS, 4 * half + 4)
                transpose(ps[0:16, 0:128], mx[:, r, 16 * half:16 * half + 16], ident[:, :]).then_inc(mx_in_psum, 1)

            def scores_for_exp(st, g):
                r = st.ring(S_ATT)
                if g % 4 == 0:
                    st.wait_dma(pe, neg_placed[g // 4], S_ATT, 16)
                st.wait(pe, exp_done, S_ATT, GROUPS, g - 1)
                mm(ps_exp[g % 2][:, :], k_stack[:, r, g, :], q_diag[:, r, g, :]).then_inc(exp_scores, 1)

            def weigh_values(st, g, stage):
                r = st.ring(stage)
                st.wait(pe, exp_done, stage, GROUPS, g + 1)
                if g == 0:
                    st.wait(pe, v_ready, stage, 1, 1)
                    st.wait(pe, av_copied, stage, 1, 0)
                region = g // VREG
                ps = ps_av[:, 128 * region:128 * region + 128]
                for i in range(4):
                    ins = mm(ps[32 * i:32 * i + 32, :], v_strip[:, r, 4 * g + i, :], expo[:, g % EXPO, 128 * i:128 * i + 128],
                             g % VREG == 0, g % VREG == VREG - 1 or g == GROUPS - 1)
                ins.then_inc(av_done, 1)

            def transpose_av(st):
                ps, r = claim(st, AT1), st.ring(S_OUT)
                st.wait(pe, av_copied, S_OUT, 1, 1)
                for c in range(3):
                    ins = transpose(ps[:, 128 * c:128 * c + 128], av[:, r, 128 * c:128 * c + 128], ident[:, :])
                ins.then_inc(attn_in_psum, 1)

            def transpose_attn(st):
                ps, r = claim(st, AT2), st.ring(S_OUT)
                st.wait(pe, attn_ready, S_OUT, 1, 1)
                for c in range(DC):
                    ins = transpose(ps[:, 128 * c:128 * c + 128], attn[:, r, 128 * c:128 * c + 128], ident[:, :])
                ins.then_inc(attnT_in_psum, 1)

            def project_out(st):
                ps, r = claim(st, WO), st.ring(S_OUT)
                st.wait(pe, attnT_ready, S_OUT, 1, 1)
                for c in range(DC):
                    ins = mm(ps[:, 0:DIM], attnT[:, r, 128 * c:128 * c + 128], wout[:, c, :], c == 0, c == DC - 1)
                ins.then_inc(wo_in_psum, 1)

            def transpose_xq(st):
                ps, r = claim(st, XQ), st.ring(S_FFN)
                st.wait(pe, xq_ready, S_FFN, 1, 1)
                for c in range(DC):
                    ins = transpose(ps[:, 64 * c:64 * c + 64].bitcast(BF16), xq[:, r, 128 * c:128 * c + 128],
                                    ident_bf[:, :])
                ins.then_inc(xqT_in_psum, 1)

            def hidden(st, half, piece):
                ps, r = claim(st, piece), st.ring(S_FFN)
                if not st.looped and st.s == S_FFN and half == 0:
                    pe.wait_ge(bias_ready, 2)
                mm(ps[:, :], b1_stack[:, :], chunk_ones[:, 4 * half:4 * half + 4, :].rearrange("p f t -> p (f t)"),
                   True, False)
                st.wait(pe, xqT_ready, S_FFN, 1, 1)
                for f in range(4):
                    for c in range(DC):
                        ins = mm(ps[:, 128 * f:128 * f + 128], w1T[:, c, 4 * half + f, :],
                                 xqT[:, r, 128 * c:128 * c + 128], False, c == DC - 1)
                ins.then_inc(h_in_psum, 1)

            def project_y(st):
                ps, r = claim(st, YY), st.ring(S_FFN)
                st.wait(pe, hq_ready, S_FFN, 2, 2)
                for f in range(FC):
                    ins = mm(ps[:, 0:DIM], hq[:, r, f, :], w2T[:, f, :], f == 0, f == FC - 1)
                ins.then_inc(y_in_psum, 1)

            def transpose_weights():
                for n in range(8):
                    which, c, quarter = n // 4, n // 2 % 2, n % 2
                    pe.wait_ge(wq_ready, which + 1)
                    if n >= 2:
                        pe.wait_ge(wT_ready[n % 2], n // 2)
                    ps = ps_exp[n % 2][:, 0:256].bitcast(BF16)
                    for f in range(4):
                        fc = 4 * quarter + f
                        at = fc * DIM + 128 * c if which == 0 else c * FFN + 128 * fc
                        ins = transpose(ps[:, 128 * f:128 * f + 128], w_q[which][:, at:at + 128], ident_bf[:, :])
                    ins.then_inc(wT_in_psum, 1)
                for n in range(2):
                    pe.wait_ge(wT_ready[n], 4)

            def body(st):
                if not st.looped and st.s == 0:
                    pe.wait_ge(id_ready, 2)
                    pe.wait_ge(ident_bf_ready, 1)
                    pe.wait_ge(early_loaded, EARLY)
                    pe.wait_ge(pads_ready, 3)
                for g in range(GROUPS):
                    if st.has(S_MAX):
                        scores_for_max(st, g)
                    if st.has(S_ATT):
                        scores_for_exp(st, g)
                    if g == 0 and st.has(S_PROJ):
                        transpose_x(st)
                    if g == 0 and st.has(S_STACK):
                        transpose_rows(st, SQ0, q_rows, q_in_psum, 1, 0)
                    if g == 1 and st.has(S_ATT):
                        transpose_maxima(st, 1, S_ATT, MX1)
                    if g == 1 and st.has(S_PROJ):
                        project_qk(st)
                    if g == 2 and st.has(S_STACK):
                        transpose_rows(st, SQ1, q_rows, q_in_psum, 1, 1)
                    if g == 2 and st.has(S_FFN):
                        transpose_xq(st)
                    if g == 3 and st.has(S_OUT):
                        transpose_av(st)
                    if g == 3 and st.has(S_FFN):
                        hidden(st, 0, H0)
                    if g == 4 and st.has(S_FFN):
                        hidden(st, 1, H1)
                    if g == 4 and st.has(S_MAX):
                        transpose_maxima(st, 0, S_MAX, MX0)
                    if g == 5 and st.has(S_OUT):
                        transpose_attn(st)
                    if g == 5 and st.has(S_PROJ):
                        project_v(st)
                    if g == 6 and st.has(S_OUT):
                        project_out(st)
                    if g == 6 and st.has(S_STACK):
                        transpose_rows(st, SK0, k_rows, k_in_psum, 2, 0)
                    if g == 7 and st.has(S_STACK):
                        transpose_rows(st, SK1, k_rows, k_in_psum, 2, 1)
                    if g == 7 and st.has(S_FFN):
                        project_y(st)
                    if g < LAG and st.has(S_OUT):
                        weigh_values(st, GROUPS - LAG + g, S_OUT)
                    if g >= LAG and st.has(S_ATT):
                        weigh_values(st, g - LAG, S_ATT)
                if not st.looped and st.s == S_ATT - 1:
                    transpose_weights()

            run_steps(pe, body)



_INS = ['x', 'ctx_1024', 'fside_BxSx2_0', 'L0_xattn_Wq', 'L0_xattn_Wkv', 'L0_xattn_Wout', 'L0_xattn_bout',
        'L0_ffn_W1', 'L0_ffn_b1', 'L0_ffn_W2', 'L0_ffn_b2', 'L0_ffn_s_act1', 'L0_ffn_s_act2']


def kernel(**inputs):
    import numpy as _np
    import concourse.bacc as _bacc
    from concourse import mybir as _mybir
    from concourse.bass_utils import run_bass_kernel_spmd as _run

    nc = _bacc.Bacc("TRN2", target_bir_lowering=False, num_devices=1)
    arrays, args = {}, []
    for name in _INS:
        a = _np.ascontiguousarray(inputs[name])
        arrays[f"in_{name}_dram"] = a
        args.append(nc.dram_tensor(f"in_{name}_dram", a.shape, _mybir.dt.from_np(a.dtype), kind="ExternalInput").ap())
    args.append(nc.dram_tensor("out_dram", (BATCH, TOK, DIM), _mybir.dt.float32, kind="ExternalOutput").ap())
    xattn_ffn_kernel(nc, *args)
    r = _run(nc, [arrays], core_ids=[0])
    return r.results[0]["out_dram"]
```

```python
import numpy as np
import concourse.bass as bass
from concourse import mybir
from contextlib import ExitStack

F32 = mybir.dt.float32
F32R = mybir.dt.float32r
BF16 = mybir.dt.bfloat16
I16 = mybir.dt.int16
I32 = mybir.dt.int32
ALU = mybir.AluOpType
ACT = mybir.ActivationFunctionType
AX = mybir.AxisListType

BATCH, TOK, DIM, CTX, HEADS, FFN = 16, 128, 256, 128, 32, 1024
HD = DIM // HEADS
GROUPS = HEADS // 4
DC = DIM // 128
FC = FFN // 128
EPS = 1e-5
SCALE = 1.0 / float(np.sqrt(np.float32(HD)))
QMIN, QMAX, HMAX = -8.0, 7.0, 15.0
ROPE_FREQ = float(np.float32(10000.0) ** np.float32(-0.5))
TWO_PI_HI = 6.28125
TWO_PI_MID = float(np.float32(2 * np.pi - 6.28125) - np.float32(2 * np.pi - 6.28125) % np.float32(2.0 ** -21))
TWO_PI_LO = float(2 * np.pi - 6.28125 - TWO_PI_MID)
SIN_LIMIT = 3.1415925

S_NORM, S_PROJ, S_STACK, S_MAX, S_ATT, S_OUT, S_FFN = range(7)
STEPS = BATCH + S_FFN
LOOP_FROM, LOOP_TO = S_FFN + 2, BATCH
XT, SQ0, MX1, QK, SQ1, XQ, AT1, H0, SK0, MX0, AT2, VV, H1, WO, SK1, YY = range(16)
PIECES = 16
PIECE_BANK = (1, 2, 0, 1, 2, 0, 1, 0, 2, 1, 0, 2, 1, 0, 2, 0)
EXPO = 4
LAG = 2
WEIGHT_SLOTS = [2 * GROUPS + 6, 2 * GROUPS + 7, 3 * GROUPS + 1, 3 * GROUPS + 4]
LOADS = ((0, 1), (1, 2), (2, 4), (4, 8), (8, 16))
NEG_ROW = 96 + 3 * HD
VREG = 3


class Step:

    def __init__(self, it, s, looped, held=None):
        self.it, self.s, self.looped = it, s, looped
        self.held = {} if held is None else held

    def value(self, per_turn, at):
        return self.held.get((per_turn, at), per_turn * self.it + at)

    def hold(self, eng, stage, per, k):
        if self.looped:
            key = (2 * per, per * (self.s - stage) + k)
            if key not in self.held:
                reg = eng.alloc_register()
                eng.reg_add(reg, key[0] * self.it, key[1])
                self.held[key] = eng.snap(reg)

    def has(self, stage):
        return self.looped or 0 <= self.s - stage < BATCH

    def ring(self, stage):
        return (self.s - stage) % 2

    def batch(self, stage):
        return self.value(2, self.s - stage) if self.looped else self.s - stage

    def wait(self, eng, sem, stage, per, k):
        at = per * (self.s - stage) + k
        if self.looped:
            assert at > 0
            eng.wait_ge(sem, self.value(2 * per, at))
        elif at > 0:
            eng.wait_ge(sem, at)

    def wait_dma(self, eng, sems, stage, per, back=0):
        sem = sems[self.ring(stage)]
        at = per * ((self.s - stage) // 2 + 1 - back)
        if self.looped:
            assert at > 0
            eng.wait_ge(sem, self.value(per, at))
        elif at > 0:
            eng.wait_ge(sem, at)


def run_steps(eng, body, hold=None):
    for s in range(LOOP_FROM):
        body(Step(0, s, False))
    with eng.Fori(0, (LOOP_TO - LOOP_FROM) // 2) as it:
        held = {}
        turn = [Step(it, LOOP_FROM + u, True, held) for u in range(2)]
        if hold:
            for st in turn:
                hold(st)
        for st in turn:
            body(st)
    for s in range(LOOP_TO, STEPS):
        body(Step(0, s, False))


def bcast(ap, axis, n):
    ap = ap.unsqueeze(axis)
    shape = list(ap.shape)
    shape[axis] = n
    return ap.broadcast_to(shape)


def xattn_ffn_kernel(nc, x, ctx_in, pos, wq_d, wkv_d, wout_d, bout_d, w1_d, b1_d, w2_d, b2_d, s1_d, s2_d, out_d):
    stack = ExitStack()
    with stack:
        def sb(name, shape, dt=F32):
            return stack.enter_context(nc.sbuf_tensor(name, shape, dt))

        def sem(name):
            return stack.enter_context(nc.semaphore(name))

        def sems(name, n=2):
            return [sem(f"{name}{i}") for i in range(n)]

        EARLY, LATE = 16 * 3, 16 * 6

        ident = sb("ident", [128, 128])
        ident_bf = sb("ident_bf", [128, 128], BF16)
        zeros = sb("zeros", [128, HD])
        minus_half = sb("minus_half", [128, 1])
        wq = sb("wq", [128, DC, DIM])
        wkv = sb("wkv", [128, 2 * DIM])
        wout = sb("wout", [128, DC, DIM])
        wq_hi = sb("wq_hi", [128, DC, DIM], F32R)
        wkv_hi = sb("wkv_hi", [128, 2 * DIM], F32R)
        wout_hi = sb("wout_hi", [128, DC, DIM], F32R)
        wq_lo = sb("wq_lo", [128, DC, DIM], F32R)
        wkv_lo = sb("wkv_lo", [128, 2 * DIM], F32R)
        wout_lo = sb("wout_lo", [128, DC, DIM], F32R)
        bout = sb("bout", [128, DIM])
        b2 = sb("b2", [128, DIM])
        b2i = sb("b2i", [128, DIM], I32)
        b2q = sb("b2q", [128, DIM])
        b1 = sb("b1", [128, FC])
        b1i = sb("b1i", [128, FC], I32)
        b1q = sb("b1q", [128, FC])
        w1 = sb("w1", [128, FC, DIM])
        w2 = sb("w2", [128, DC, FFN])
        w_i = [sb("w1_i", [128, 2048], I16), sb("w2_i", [128, 2048], I16)]
        w_q = [w_i[0][:, :].bitcast(BF16), w_i[1][:, :].bitcast(BF16)]
        w1T = sb("w1T", [128, DC, FC, 128], BF16)
        w2T = sb("w2T", [128, FC, DIM], BF16)
        s_act = sb("s_act", [128, 2])
        r_act = sb("r_act", [128, 2])
        wmax = sb("wmax", [128, 2])
        wmax_all = sb("wmax_all", [128, 2])
        r_wmax = sb("r_wmax", [128, 2])
        w_levels = sb("w_levels", [128, 2])
        w_scale = sb("w_scale", [128, 2])
        h_scale = sb("h_scale", [128, 2])
        r_h_scale = sb("r_h_scale", [128, 2])
        relu_scale = sb("relu_scale", [128, 1])
        n_ang = BATCH * 4
        x_all = sb("x_all", [128, BATCH, DIM])
        c_in = sb("c_in", [128, 2, CTX])
        pos_sb = sb("pos_sb", [128, BATCH, 2])
        ang = sb("ang", [128, BATCH, 2, 2])
        turns = sb("turns", [128, 2, n_ang], I32)
        red = sb("red", [128, 4, 2, n_ang])
        trig = sb("trig", [128, 2, n_ang])
        cos8 = sb("cos8", [128, BATCH, 4, 2])
        sin_neg = sb("sin_neg", [128, BATCH, 4])
        sin_pos = sb("sin_pos", [128, BATCH, 4])
        bn1 = sb("bn1", [128, 2, 6])
        mv1 = sb("mv1", [128, 2, 2])
        var1 = sb("var1", [128, 2, 1])
        rstd1 = sb("rstd1", [128, 2, 1])
        xn = sb("xn", [128, 2, DIM])
        xT_hi = sb("xT_hi", [128, 2, DIM + CTX], F32R)
        xT_lo = sb("xT_lo", [128, 2, DIM + CTX], F32R)
        by_cos = sb("by_cos", [128, 2 * DIM])
        by_sin = sb("by_sin", [128, 2 * DIM])
        rot = sb("rot", [128, 2, 2 * DIM])
        q_rows = sb("q_rows", [128, 2, HEADS, 32])
        k_rows = sb("k_rows", [128, 2, HEADS, 32])
        q_comp = sb("q_comp", [128, 2, GROUPS, 128], F32R)
        k_stack = sb("k_stack", [128, 2, GROUPS, 128], F32R)
        q_diag = sb("q_diag", [128, 2, GROUPS, 512], F32R)
        v_comp = sb("v_comp", [128, 2, DIM])
        v_strip = sb("v_strip", [128, 2, HEADS, 32])
        mx = sb("mx", [128, 2, HEADS])
        mxT = sb("mxT", [16, 2, 2, 128], F32R)
        expo = sb("expo", [128, EXPO, 512])
        av = sb("av", [128, 2, 384])
        r_sum = sb("r_sum", [128, 2, 3 * VREG * 4])
        attn = sb("attn", [128, 2, DIM])
        attnT_hi = sb("attnT_hi", [128, 2, DIM], F32R)
        attnT_lo = sb("attnT_lo", [128, 2, DIM], F32R)
        x_b = sb("x_b", [128, 2, DIM])
        x2 = sb("x2", [128, 2, DIM])
        bn2 = sb("bn2", [128, 2, 6])
        mv2 = sb("mv2", [128, 2, 2])
        var2 = sb("var2", [128, 2, 1])
        rstd2 = sb("rstd2", [128, 2, 1])
        xn2 = sb("xn2", [128, 2, DIM])
        xq_i = sb("xq_i", [128, 2, DIM], I16)
        xq = sb("xq", [128, 2, DIM], BF16)
        xqT = sb("xqT", [128, 2, DIM], BF16)
        h_i = sb("h_i", [128, 2, FC, 128], I16)
        hq = sb("hq", [128, 2, FC, 128], BF16)
        x2_b = sb("x2_b", [128, 2, DIM])
        y = sb("y", [128, 2, DIM])

        def bank(name):
            return stack.enter_context(nc.psum_tensor(name, [128, 512], F32))

        ps_max = [bank("ps_max0"), bank("ps_max1")]
        ps_exp = [bank("ps_exp0"), bank("ps_exp1")]
        ps_av = bank("ps_av")
        ps_misc = [bank(f"ps_misc{n}") for n in range(3)]

        loaded = sems("loaded", len(LOADS))
        c_loaded = sems("c_loaded")
        stored = sem("stored")
        early_loaded = sem("early_loaded")
        w_loaded = sem("w_loaded")
        pos_loaded = sem("pos_loaded")
        late_loaded = sem("late_loaded")
        diag_placed = [sems("diag_placed_lo"), sems("diag_placed_hi")]
        neg_placed = [sems("neg_placed_lo"), sems("neg_placed_hi")]
        id_ready = sem("id_ready")
        rope_step = sem("rope_step")
        ang_ready = sem("ang_ready")
        trig_ready = sem("trig_ready")
        wprep = sem("wprep")
        bias_ready = sem("bias_ready")
        wmax_ready = sem("wmax_ready")
        wmax_shared = sem("wmax_shared")
        wq_ready = sem("wq_ready")
        wT_in_psum = sem("wT_in_psum")
        wT_ready = sems("wT_ready")
        pads_ready = sem("pads_ready")
        zeros_ready = sem("zeros_ready")
        strips_ready = sem("strips_ready")
        ident_bf_ready = sem("ident_bf_ready")
        ln1_step = sem("ln1_step")
        var1_ready = sem("var1_ready")
        rstd1_ready = sem("rstd1_ready")
        xn_ready = sem("xn_ready")
        xT_in_psum = sem("xT_in_psum")
        xT_hi_ready = sem("xT_hi_ready")
        xT_lo_ready = sem("xT_lo_ready")
        w_hi_ready = sem("w_hi_ready")
        w_lo_ready = sem("w_lo_ready")
        qk_in_psum = sem("qk_in_psum")
        rope_terms = sem("rope_terms")
        rot_ready = sem("rot_ready")
        hi_ready = sem("hi_ready")
        lo_ready = sem("lo_ready")
        v_in_psum = sem("v_in_psum")
        v_copied = sem("v_copied")
        v_ready = sem("v_ready")
        q_in_psum = sem("q_in_psum")
        q_ready = sem("q_ready")
        k_in_psum = sem("k_in_psum")
        k_ready = sem("k_ready")
        max_scores = sem("max_scores")
        max_done = sem("max_done")
        mx_in_psum = sem("mx_in_psum")
        mxT_ready = sem("mxT_ready")
        exp_scores = sem("exp_scores")
        exp_done = sem("exp_done")
        av_done = sem("av_done")
        av_copied = sem("av_copied")
        attn_in_psum = sem("attn_in_psum")
        r_sum_ready = sem("r_sum_ready")
        attn_ready = sem("attn_ready")
        attnT_in_psum = sem("attnT_in_psum")
        attnT_hi_ready = sem("attnT_hi_ready")
        attnT_lo_ready = sem("attnT_lo_ready")
        wo_in_psum = sem("wo_in_psum")
        x_b_ready = sem("x_b_ready")
        x2_ready = sem("x2_ready")
        ln2_step = sem("ln2_step")
        var2_ready = sem("var2_ready")
        rstd2_ready = sem("rstd2_ready")
        xq_step = sem("xq_step")
        xq_ready = sem("xq_ready")
        xqT_in_psum = sem("xqT_in_psum")
        xqT_ready = sem("xqT_ready")
        h_in_psum = sem("h_in_psum")
        relu_done = sem("relu_done")
        hq_ready = sem("hq_ready")
        y_in_psum = sem("y_in_psum")
        x2_b_ready = sem("x2_b_ready")
        y_ready = sem("y_ready")

        block = stack.enter_context(nc.Block())

        def copy_wT(eng, n):
            src = ps_exp[n % 2][:, 0:256].bitcast(BF16).rearrange("p (f c) -> p f c", f=4)
            which, c, quarter = n // 4, n // 2 % 2, n % 2
            fs = slice(4 * quarter, 4 * quarter + 4)
            dst = w1T[:, c, fs, :] if which == 0 else w2T[:, fs, 128 * c:128 * c + 128]
            eng.wait_ge(wT_in_psum, n + 1)
            copy = eng.tensor_copy if eng is nc.vector else eng.copy
            copy(dst, src).then_inc(wT_ready[n % 2], 1)

        w_flat = [w1[:, :, :].rearrange("p c d -> p (c d)"), w2[:, :, :].rearrange("p c f -> p (c f)")]
        out_pairs = out_d.rearrange("(k two) t d -> k t two d", two=2)

        def norm_early(st):
            return not st.looped and st.s < 4

        def wait_loaded(eng, st, stage):
            if not st.looped:
                b = st.s - stage
                for n, (lo, hi) in enumerate(LOADS):
                    if lo == b or (st.s == LOOP_FROM - 1 and lo > b):
                        eng.wait_ge(loaded[n], 16)

        def all_rows(ap):
            return bcast(ap, 0, 128)

        @block.sync
        def _(sp):
            def load(n):
                lo, hi = LOADS[n]
                sp.dma_start(x_all[:, lo:hi, :], x[lo:hi].rearrange("b t d -> t b d")).then_inc(loaded[n], 16)

            def load_context(st):
                r, b = st.ring(S_NORM), st.batch(S_NORM)
                st.wait(sp, xT_in_psum, S_NORM, 1, -1)
                sp.dma_start(c_in[:, r, :], ctx_in[b]).then_inc(c_loaded[r], 16)

            def place_queries(st, half):
                r = st.ring(S_STACK)
                gs = slice(4 * half, 4 * half + 4)
                st.wait(sp, q_ready, S_STACK, 2, half + 1)
                st.wait(sp, exp_scores, S_STACK, GROUPS, 4 * half + 4 - 2 * GROUPS)
                if not st.looped and half == 0 and st.s < S_STACK + 2:
                    sp.wait_ge(zeros_ready, r + 1)
                for j in range(4):
                    rows, cols = slice(32 * j, 32 * j + 32), slice(128 * j, 128 * j + 128)
                    sp.dma_start(q_diag[rows, r, gs, cols].bitcast(F32), q_comp[rows, r, gs, :].bitcast(F32))\
                      .then_inc(diag_placed[half][r], 16)

            def place_maxima(st, half, stage):
                r = st.ring(stage)
                st.wait(sp, mxT_ready, stage, 2, half + 1)
                dst = q_diag[NEG_ROW:NEG_ROW + 1, r, 4 * half:4 * half + 4, :].rearrange("o g (j t) -> o (g j) t", j=4)
                sp.dma_start(dst.bitcast(F32), mxT[:, r, half, :].bitcast(F32)).then_inc(neg_placed[half][r], 16)

            def store(st):
                st.wait(sp, y_ready, S_FFN, 1, 1)
                pair = st.value(1, (st.s - S_FFN) // 2)
                sp.dma_start(out_pairs[pair], y[:, :, :]).then_inc(stored, 16)

            def body(st):
                if st.has(S_NORM) and st.s > 1:
                    load_context(st)
                if not st.looped and st.s in (2, 4):
                    load(3 if st.s == 2 else 4)
                if st.has(S_ATT):
                    place_maxima(st, 1, S_ATT)
                if st.has(S_STACK):
                    place_queries(st, 0)
                if st.has(S_MAX):
                    place_maxima(st, 0, S_MAX)
                if st.has(S_STACK):
                    place_queries(st, 1)
                if st.has(S_FFN) and st.ring(S_FFN) == 1:
                    store(st)

            load(0)
            load_context(Step(0, 0, False))
            for c in range(DC):
                sp.dma_start(wq[:, c, :], wq_d[128 * c:128 * c + 128, :]).then_inc(early_loaded, 16)
            sp.dma_start(wkv[:, :], wkv_d).then_inc(early_loaded, 16)
            load(1)
            load_context(Step(0, 1, False))
            sp.dma_start(w1[:, :, :], w1_d.rearrange("(c p) d -> p c d", p=128)).then_inc(w_loaded, 16)
            sp.dma_start(w2[:, :, :], w2_d.rearrange("(c p) f -> p c f", p=128)).then_inc(w_loaded, 16)
            load(2)
            late = [
                (wout[:, :, :], wout_d.rearrange("(c p) d -> p c d", p=128)),
                (b1[:, :], b1_d.rearrange("(c p) -> p c", p=128)),
                (bout[:, :], all_rows(bout_d)),
                (b2[:, :], all_rows(b2_d)),
                (s_act[:, 0:1], all_rows(s1_d)),
                (s_act[:, 1:2], all_rows(s2_d)),
            ]
            for dst, src in late:
                sp.dma_start(dst, src, allow_slow_non_contiguous=True).then_inc(late_loaded, 16)

            def hold(st):
                for half in range(2):
                    st.hold(sp, S_STACK, GROUPS, 4 * half + 4 - 2 * GROUPS)

            run_steps(sp, body, hold)
            sp.wait_ge(stored, 16 * BATCH // 2)

        @block.gpsimd
        def _(pool):
            pool.memset(ident[:, :], 0.0).then_inc(id_ready, 1)
            pool.wait_ge(id_ready, 1)
            pool.affine_select(out=ident[:, :], in_=ident[:, :], compare_op=ALU.not_equal, fill=1.0,
                               base=0, pattern=[[-1, 128]], channel_multiplier=1).then_inc(id_ready, 1)
            pool.memset(zeros[:, :], 0.0).then_inc(id_ready, 1)
            pool.memset(minus_half[:, :], -0.5).then_inc(id_ready, 1)
            pool.wait_ge(id_ready, 4)
            pool.memset(q_rows[:, :, :, :], 0.0).then_inc(pads_ready, 1)
            pool.memset(k_rows[:, :, :, :], 0.0).then_inc(pads_ready, 1)
            pool.wait_ge(pads_ready, 2)
            pool.memset(k_rows[:, :, NEG_ROW // 32::4, NEG_ROW % 32:NEG_ROW % 32 + 1], -1.0).then_inc(pads_ready, 1)

            def split_weight(n, lo, full, hi):
                pool.wait_ge(w_hi_ready, n + 1)
                pool.tensor_tensor(lo, full, hi, ALU.subtract).then_inc(w_lo_ready, 1)

            def clear_diagonal(r):
                pool.memset(q_diag[:, r, :, :].bitcast(I32), 0).then_inc(zeros_ready, 1)

            def fill_strips():
                pool.memset(v_strip[:, :, :, :], 0.0).then_inc(strips_ready, 1)
                pool.wait_ge(strips_ready, 1)
                for s in range(VREG):
                    for g in range(s, GROUPS, VREG):
                        ins = pool.memset(v_strip[:, :, 4 * g:4 * g + 4, 9 * s + HD:9 * s + HD + 1], 1.0)
                ins.then_inc(strips_ready, 1)

            def norm(st):
                r = st.ring(S_NORM)
                st.wait(pool, var1_ready, S_NORM, 1, 1)
                st.wait(pool, xn_ready, S_NORM, 1, -1)
                pool.tensor_tensor(rstd1[:, r, :], var1[:, r, :], minus_half[:, :], ALU.pow).then_inc(rstd1_ready, 1)

            def rotate(st):
                r = st.ring(S_PROJ)
                st.wait(pool, rope_terms, S_PROJ, 3, 3)
                st.wait(pool, hi_ready, S_PROJ, 2, -2)
                st.wait(pool, lo_ready, S_PROJ, 2, -2)
                pool.tensor_tensor(rot[:, r, :], by_cos[:, :], by_sin[:, :], ALU.add).then_inc(rot_ready, 1)

            def split_low(st, n):
                r = st.ring(S_PROJ)
                rows, at = (q_rows, k_rows)[n], (16, 8)[n]
                st.wait(pool, hi_ready, S_PROJ, 2, n + 1)
                src = rot[:, r, n * DIM:(n + 1) * DIM].rearrange("p (h d) -> p h d", d=HD)
                pool.tensor_tensor(rows[:, r, :, at:at + HD], src, rows[:, r, :, 0:HD], ALU.subtract)\
                    .then_inc(lo_ready, 1)

            def place_values(st):
                r = st.ring(S_MAX)
                st.wait(pool, v_copied, S_MAX, 1, 1)
                st.wait(pool, av_done, S_MAX, GROUPS, -GROUPS)
                if not st.looped and st.s == S_MAX:
                    pool.wait_ge(strips_ready, 2)
                for region in range(3):
                    n = min(VREG, GROUPS - VREG * region)
                    h = 4 * VREG * region
                    strips = v_strip[:, r, h:h + 4 * n, :].rearrange("p (s i) c -> p s i c", s=n)
                    for s in range(n):
                        vals = v_comp[:, r, (h + 4 * s) * HD:(h + 4 * s + 4) * HD].rearrange("p (i d) -> p i d", d=HD)
                        nothing = bcast(zeros[:, 0:HD], 1, 4)
                        ins = pool.tensor_tensor(strips[:, s, :, 9 * s:9 * s + HD], vals, nothing, ALU.add)
                ins.then_inc(v_ready, 1)

            def residual_bias(st):
                r = st.ring(S_ATT)
                wait_loaded(pool, st, S_ATT)
                if not st.looped and st.s == S_ATT:
                    pool.wait_ge(late_loaded, LATE)
                st.wait(pool, x2_ready, S_ATT, 1, -1)
                pool.tensor_tensor(x_b[:, r, :], x_all[:, st.batch(S_ATT), :], bout[:, :], ALU.add).then_inc(x_b_ready, 1)

            def norm2(st):
                r = st.ring(S_OUT)
                st.wait(pool, var2_ready, S_OUT, 1, 1)
                st.wait(pool, xq_ready, S_OUT, 1, -1)
                pool.tensor_tensor(rstd2[:, r, :], var2[:, r, :], minus_half[:, :], ALU.pow).then_inc(rstd2_ready, 1)

            def output_bias(st):
                r = st.ring(S_OUT)
                st.wait(pool, x2_ready, S_OUT, 1, 1)
                st.wait(pool, y_ready, S_OUT, 1, -1)
                pool.tensor_tensor(x2_b[:, r, :], x2[:, r, :], b2q[:, :], ALU.add).then_inc(x2_b_ready, 1)

            def body(st):
                if not st.looped and st.s == S_OUT:
                    pool.wait_ge(bias_ready, 2)
                if st.has(S_MAX):
                    place_values(st)
                if st.has(S_ATT):
                    residual_bias(st)
                if st.has(S_NORM) and norm_early(st):
                    norm(st)
                if not st.looped and st.s == 2:
                    pool.wait_ge(wmax_ready, 2)
                    pool.partition_all_reduce(wmax_all[:, :], wmax[:, :], 128, bass.bass_isa.ReduceOp.max)\
                        .then_inc(wmax_shared, 1)
                if st.has(S_PROJ):
                    rotate(st)
                if st.has(S_NORM) and not norm_early(st):
                    norm(st)
                if st.has(S_PROJ):
                    split_low(st, 0)
                    split_low(st, 1)
                if not st.looped and st.s == 0:
                    split_weight(0, wq_lo[:, :, :], wq[:, :, :], wq_hi[:, :, :].bitcast(F32))
                    split_weight(1, wkv_lo[:, :], wkv[:, :], wkv_hi[:, :].bitcast(F32))
                if not st.looped and st.s == 3:
                    split_weight(2, wout_lo[:, :, :], wout[:, :, :], wout_hi[:, :, :].bitcast(F32))
                if not st.looped and st.s in (0, 2):
                    clear_diagonal(st.s // 2)
                if not st.looped and st.s == 1:
                    fill_strips()
                if st.has(S_OUT):
                    norm2(st)
                    output_bias(st)

            run_steps(pool, body)

        @block.scalar
        def _(act):
            act.dma_start(pos_sb[:, :, :], pos.rearrange("b t p -> t b p")).then_inc(pos_loaded, 16)
            act.wait_ge(id_ready, 2)
            act.copy(ident_bf[:, :], ident[:, :]).then_inc(ident_bf_ready, 1)
            act.wait_ge(early_loaded, EARLY)
            act.copy(wq_hi[:, :, :], wq[:, :, :]).then_inc(w_hi_ready, 1)
            act.copy(wkv_hi[:, :], wkv[:, :]).then_inc(w_hi_ready, 1)

            def copy_xT(st):
                r = st.ring(S_PROJ)
                st.wait(act, xT_in_psum, S_PROJ, 1, 1)
                st.wait(act, v_in_psum, S_PROJ, 1, -1)
                act.copy(xT_hi[:, r, :], ps_misc[PIECE_BANK[XT]][:, 0:DIM + CTX]).then_inc(xT_hi_ready, 1)

            def split_high(st, n):
                r = st.ring(S_PROJ)
                st.wait(act, rot_ready, S_PROJ, 1, 1)
                if not st.looped and st.s == S_PROJ:
                    act.wait_ge(pads_ready, 3)
                st.wait(act, (q_in_psum, k_in_psum)[n], S_PROJ, 2, -2)
                src = bcast(rot[:, r, n * DIM:(n + 1) * DIM].rearrange("p (h d) -> p h d", d=HD), 2, 2)
                rows = (q_rows, k_rows)[n][:, r, :, :].bitcast(F32R).rearrange("p h (c d) -> p h c d", d=HD)
                act.copy(rows[:, :, 0:2, :] if n == 0 else rows[:, :, 0:3:2, :], src).then_inc(hi_ready, 1)

            def copy_v(st):
                r = st.ring(S_PROJ)
                st.wait(act, v_in_psum, S_PROJ, 1, 1)
                st.wait(act, v_ready, S_PROJ, 1, -1)
                act.copy(v_comp[:, r, :], ps_misc[PIECE_BANK[VV]][:, 0:DIM]).then_inc(v_copied, 1)

            def copy_queries(st, half):
                r = st.ring(S_STACK)
                st.wait(act, q_in_psum, S_STACK, 2, half + 1)
                st.wait_dma(act, diag_placed[half], S_STACK, 64, back=1)
                src = ps_misc[PIECE_BANK[(SQ0, SQ1)[half]]][:, :].rearrange("p (g t) -> p g t", g=4)
                act.copy(q_comp[:, r, 4 * half:4 * half + 4, :], src).then_inc(q_ready, 1)

            def copy_keys(st, half):
                r = st.ring(S_STACK)
                st.wait(act, k_in_psum, S_STACK, 2, half + 1)
                st.wait(act, exp_scores, S_STACK, GROUPS, 4 * half + 4 - 2 * GROUPS)
                act.copy(k_stack[:, r, 4 * half:4 * half + 4, :],
                         ps_misc[PIECE_BANK[(SK0, SK1)[half]]][:, :].rearrange("p (g t) -> p g t", g=4)).then_inc(k_ready, 1)

            def exponentials(st, g):
                st.wait(act, exp_scores, S_ATT, GROUPS, g + 1)
                st.wait(act, av_done, S_ATT, GROUPS, g + 1 - EXPO)
                act.activation(expo[:, g % EXPO, :], ps_exp[g % 2][:, :], ACT.Exp, scale=SCALE).then_inc(exp_done, 1)

            def copy_av(st):
                r = st.ring(S_OUT)
                st.wait(act, av_done, S_OUT, GROUPS, GROUPS)
                st.wait(act, attn_in_psum, S_OUT, 1, -1)
                act.copy(av[:, r, :], ps_av[:, 0:384]).then_inc(av_copied, 1)

            def copy_attnT(st):
                r = st.ring(S_OUT)
                st.wait(act, attnT_in_psum, S_OUT, 1, 1)
                st.wait(act, wo_in_psum, S_OUT, 1, -1)
                act.copy(attnT_hi[:, r, :], ps_misc[PIECE_BANK[AT2]][:, 0:DIM]).then_inc(attnT_hi_ready, 1)

            def copy_xqT(st):
                r = st.ring(S_FFN)
                st.wait(act, xqT_in_psum, S_FFN, 1, 1)
                st.wait(act, h_in_psum, S_FFN, 2, -2)
                act.copy(xqT[:, r, :], ps_misc[PIECE_BANK[XQ]][:, 0:DIM // 2].bitcast(BF16)).then_inc(xqT_ready, 1)

            def relu(st, half):
                r = st.ring(S_FFN)
                st.wait(act, h_in_psum, S_FFN, 2, half + 1)
                st.wait(act, hq_ready, S_FFN, 2, half - 3)
                if not st.looped and st.s == S_FFN and half == 0:
                    act.wait_ge(bias_ready, 2)
                for c in range(4):
                    f = 4 * half + c
                    ins = act.activation(h_i[:, r, f, :], ps_misc[PIECE_BANK[(H0, H1)[half]]][:, 128 * c:128 * c + 128],
                                         ACT.Relu, bias=b1q[:, f:f + 1], scale=relu_scale[:, :])
                ins.then_inc(relu_done, 1)

            def body(st):
                for g in range(GROUPS):
                    if g == LAG and st.has(S_OUT):
                        copy_av(st)
                    if g == 0 and st.has(S_PROJ):
                        copy_xT(st)
                    if g == 4 and st.has(S_STACK):
                        copy_keys(st, 0)
                    if g == 5 and st.has(S_OUT):
                        copy_attnT(st)
                    if st.has(S_ATT):
                        exponentials(st, g)
                    if g == 0 and st.has(S_STACK):
                        copy_queries(st, 0)
                    if g == 0 and not st.looped and st.s == S_PROJ:
                        act.wait_ge(ang_ready, 1)
                        act.activation(trig[:, :, :], red[:, 3, :, :], ACT.Sin).then_inc(trig_ready, 1)
                    if g == 3 and not st.looped and st.s == 3:
                        act.wait_ge(late_loaded, LATE)
                        act.copy(wout_hi[:, :, :], wout[:, :, :]).then_inc(w_hi_ready, 1)
                    before = st.s * GROUPS + g - 1
                    if not st.looped and before in WEIGHT_SLOTS:
                        copy_wT(act, 2 * WEIGHT_SLOTS.index(before) + 1)
                    if g == 2 and st.has(S_FFN):
                        copy_xqT(st)
                    if g == 2 and st.has(S_STACK):
                        copy_queries(st, 1)
                    if g == 3 and st.has(S_FFN):
                        relu(st, 0)
                    if g == 5 and st.has(S_PROJ):
                        copy_v(st)
                    if g == 5 and st.has(S_FFN):
                        relu(st, 1)
                    if g in (6, 7) and st.has(S_PROJ):
                        split_high(st, g - 6)
                    if g == 6 and st.has(S_STACK):
                        copy_keys(st, 1)

            run_steps(act, body)

        @block.vector
        def _(dve):
            steps = [0]

            def link(ins, chain):
                steps[0] += 1
                ins.then_inc(chain, 1)
                dve.wait_ge(chain, steps[0])

            def rope_tables():
                dve.wait_ge(pos_loaded, 16)
                for f, freq in enumerate((1.0, ROPE_FREQ)):
                    link(dve.tensor_scalar(ang[:, :, :, f], pos_sb[:, :, :], freq, None, ALU.mult), rope_step)
                angles = ang[:, :, :, :].rearrange("p b a f -> p (b a f)")
                for n in range(2):
                    link(dve.tensor_scalar(turns[:, n, :], angles, 1.0 / (2 * np.pi), 0.25 * n, ALU.mult, ALU.add), rope_step)
                    link(dve.tensor_copy(red[:, 0, n, :], turns[:, n, :]), rope_step)
                    link(dve.scalar_tensor_tensor(out=red[:, 1, n, :], in0=red[:, 0, n, :], scalar=-TWO_PI_HI, in1=angles,
                                                  op0=ALU.mult, op1=ALU.add), rope_step)
                    link(dve.scalar_tensor_tensor(out=red[:, 2, n, :], in0=red[:, 0, n, :], scalar=-TWO_PI_MID,
                                                  in1=red[:, 1, n, :], op0=ALU.mult, op1=ALU.add), rope_step)
                    link(dve.scalar_tensor_tensor(out=red[:, 1, n, :], in0=red[:, 0, n, :], scalar=-TWO_PI_LO,
                                                  in1=red[:, 2, n, :], op0=ALU.mult, op1=ALU.add), rope_step)
                    link(dve.tensor_scalar(red[:, 2, n, :], red[:, 1, n, :], 0.5 * np.pi * n, SIN_LIMIT, ALU.add, ALU.min),
                         rope_step)
                    link(dve.tensor_scalar(red[:, 3, n, :], red[:, 2, n, :], -SIN_LIMIT, None, ALU.max), rope_step)
                dve.wait_ge(rope_step, steps[0])
                dve.tensor_copy(red[:, 0, 0, 0:1], red[:, 3, 0, 0:1]).then_inc(ang_ready, 1)

            def spread_tables():
                dve.wait_ge(trig_ready, 1)
                sine = trig[:, 0, :].rearrange("p (b f) -> p b f", b=BATCH)
                cosine = trig[:, 1, :].rearrange("p (b f) -> p b f", b=BATCH)
                dve.tensor_copy(cos8[:, :, :, 0], cosine)
                dve.tensor_copy(cos8[:, :, :, 1], cosine)
                dve.tensor_scalar(sin_neg[:, :, :], sine, -1.0, None, ALU.mult)
                link(dve.tensor_copy(sin_pos[:, :, :], sine), rope_step)

            def weight_maxima(n):
                dve.wait_ge(w_loaded, 32)
                dve.tensor_reduce(out=wmax[:, n:n + 1], in_=w_flat[n], axis=AX.X, op=ALU.max,
                                  apply_absolute_value=True).then_inc(wmax_ready, 1)

            def prepare_levels():
                steps[0] = 0
                dve.wait_ge(wmax_shared, 1)
                link(dve.reciprocal(r_wmax[:, :], wmax_all[:, :]), wprep)
                link(dve.tensor_scalar(w_levels[:, :], r_wmax[:, :], QMAX, None, ALU.mult), wprep)

            def quantise_weights(n):
                link(dve.tensor_scalar(w_i[n][:, :], w_flat[n], w_levels[:, n:n + 1], None, ALU.mult), wprep)
                dve.tensor_scalar(w_q[n][:, :], w_i[n][:, :], QMIN, QMAX, ALU.max, ALU.min).then_inc(wq_ready, 1)

            def prepare_scales():
                dve.wait_ge(late_loaded, LATE)
                link(dve.reciprocal(r_act[:, :], s_act[:, :]), wprep)
                link(dve.tensor_scalar(w_scale[:, :], wmax_all[:, :], 1.0 / QMAX, None, ALU.mult), wprep)
                link(dve.tensor_tensor(h_scale[:, :], w_scale[:, :], s_act[:, :], ALU.mult), wprep)
                link(dve.reciprocal(r_h_scale[:, :], h_scale[:, :]), wprep)
                link(dve.tensor_tensor(relu_scale[:, :], h_scale[:, 0:1], r_act[:, 1:2], ALU.mult), wprep)

            def round_b2():
                link(dve.tensor_scalar(b2i[:, :], b2[:, :], r_h_scale[:, 1:2], None, ALU.mult), wprep)
                dve.tensor_scalar(b2q[:, :], b2i[:, :], h_scale[:, 1:2], None, ALU.mult).then_inc(bias_ready, 1)

            def round_b1():
                link(dve.tensor_scalar(b1i[:, :], b1[:, :], r_h_scale[:, 0:1], None, ALU.mult), wprep)
                dve.tensor_scalar(b1q[:, :], b1i[:, :], relu_scale[:, :], None, ALU.mult).then_inc(bias_ready, 1)

            def norm1_stats(st):
                r = st.ring(S_NORM)
                wait_loaded(dve, st, S_NORM)
                dve.bn_stats(bn1[:, r, :], x_all[:, st.batch(S_NORM), :]).then_inc(ln1_step, 1)

            def norm1_moments(st):
                r = st.ring(S_NORM)
                dve.bn_aggr(mv1[:, r, :], bn1[:, r, :]).then_inc(ln1_step, 1)

            def norm1_variance(st):
                r = st.ring(S_NORM)
                st.wait(dve, ln1_step, S_NORM, 2, 2)
                st.wait(dve, rstd1_ready, S_NORM, 1, -1)
                dve.tensor_scalar(var1[:, r, :], mv1[:, r, 1:2], EPS, None, ALU.add).then_inc(var1_ready, 1)

            def norm1(st):
                r = st.ring(S_NORM)
                st.wait(dve, rstd1_ready, S_NORM, 1, 1)
                st.wait(dve, xT_in_psum, S_NORM, 1, -1)
                dve.tensor_scalar(xn[:, r, :], x_all[:, st.batch(S_NORM), :], mv1[:, r, 0:1], rstd1[:, r, :],
                                  ALU.subtract, ALU.mult).then_inc(xn_ready, 1)

            def split_xT(st):
                r = st.ring(S_PROJ)
                st.wait(dve, xT_hi_ready, S_PROJ, 1, 1)
                st.wait(dve, v_in_psum, S_PROJ, 1, -1)
                dve.tensor_tensor(xT_lo[:, r, :], ps_misc[PIECE_BANK[XT]][:, 0:DIM + CTX],
                                  xT_hi[:, r, :].bitcast(F32), ALU.subtract).then_inc(xT_lo_ready, 1)

            def split_attnT(st):
                r = st.ring(S_OUT)
                st.wait(dve, attnT_hi_ready, S_OUT, 1, 1)
                st.wait(dve, wo_in_psum, S_OUT, 1, -1)
                dve.tensor_tensor(attnT_lo[:, r, :], ps_misc[PIECE_BANK[AT2]][:, 0:DIM],
                                  attnT_hi[:, r, :].bitcast(F32), ALU.subtract).then_inc(attnT_lo_ready, 1)

            def rope(st):
                r, b = st.ring(S_PROJ), st.batch(S_PROJ)
                st.wait(dve, qk_in_psum, S_PROJ, 1, 1)
                st.wait(dve, rot_ready, S_PROJ, 1, 0)
                ps = ps_misc[PIECE_BANK[QK]][:, :]
                cos_b = bcast(cos8[:, b, :, :].rearrange("p f c -> p (f c)"), 1, 2 * HEADS)
                dve.tensor_tensor(by_cos[:, :].rearrange("p (h d) -> p h d", d=HD),
                                  ps.rearrange("p (h d) -> p h d", d=HD), cos_b, ALU.mult).then_inc(rope_terms, 1)
                pairs_in = ps.rearrange("p (h f c) -> p h f c", f=4, c=2)
                pairs_out = by_sin[:, :].rearrange("p (h f c) -> p h f c", f=4, c=2)
                for c, s in enumerate((sin_neg, sin_pos)):
                    dve.tensor_tensor(pairs_out[:, :, :, c], pairs_in[:, :, :, 1 - c],
                                      bcast(s[:, b, :], 1, 2 * HEADS), ALU.mult).then_inc(rope_terms, 1)

            def maxima(st, g):
                r = st.ring(S_MAX)
                st.wait(dve, max_scores, S_MAX, GROUPS, g + 1)
                if g == 0:
                    st.wait(dve, mx_in_psum, S_MAX, 2, -2)
                dve.tensor_reduce(out=mx[:, r, 4 * g:4 * g + 4],
                                  in_=ps_max[g % 2][:, :].rearrange("p (h k) -> p h k", h=4),
                                  axis=AX.X, op=ALU.max).then_inc(max_done, 1)

            def copy_maxima(st, half, stage):
                r = st.ring(stage)
                st.wait(dve, mx_in_psum, stage, 2, half + 1)
                st.wait_dma(dve, neg_placed[half], stage, 16, back=1)
                dve.tensor_copy(mxT[:, r, half, :], ps_misc[PIECE_BANK[(MX0, MX1)[half]]][0:16, 0:128]).then_inc(mxT_ready, 1)

            def normalise(st):
                r = st.ring(S_OUT)
                st.wait(dve, attn_in_psum, S_OUT, 1, 1)
                st.wait(dve, attn_ready, S_OUT, 1, -1)
                st.wait(dve, attnT_in_psum, S_OUT, 1, -1)
                sums = ps_misc[PIECE_BANK[AT1]][:, 0:384].rearrange("p (r i c) -> p r i c", r=3, i=4)\
                    [:, :, :, HD::9]
                inverse = r_sum[:, r, :].rearrange("p (r s i) -> p r i s", r=3, s=VREG)
                dve.reciprocal(inverse, sums).then_inc(r_sum_ready, 1)
                st.wait(dve, r_sum_ready, S_OUT, 1, 1)
                for region in range(3):
                    n = min(VREG, GROUPS - VREG * region)
                    cols = ps_misc[PIECE_BANK[AT1]][:, 128 * region:128 * region + 128].rearrange("p (i c) -> p i c", i=4)
                    vals = cols[:, :, 0:9 * n].rearrange("p i (s d) -> p s i d", d=9)[:, :, :, 0:HD]
                    h = 4 * VREG * region
                    scale = bcast(r_sum[:, r, h:h + 4 * n].rearrange("p (s i) -> p s i", s=n), 3, HD)
                    dst = attn[:, r, h * HD:(h + 4 * n) * HD].rearrange("p (s i d) -> p s i d", s=n, d=HD)
                    ins = dve.tensor_tensor(dst, vals, scale, ALU.mult)
                ins.then_inc(attn_ready, 1)

            def residual(st):
                r = st.ring(S_OUT)
                st.wait(dve, wo_in_psum, S_OUT, 1, 1)
                st.wait(dve, x_b_ready, S_OUT, 1, 1)
                st.wait(dve, x2_b_ready, S_OUT, 1, -1)
                dve.tensor_tensor(x2[:, r, :], ps_misc[PIECE_BANK[WO]][:, 0:DIM], x_b[:, r, :], ALU.add).then_inc(x2_ready, 1)

            def norm2_stats(st):
                r = st.ring(S_OUT)
                st.wait(dve, x2_ready, S_OUT, 1, 1)
                dve.bn_stats(bn2[:, r, :], x2[:, r, :]).then_inc(ln2_step, 1)

            def norm2_moments(st):
                r = st.ring(S_OUT)
                dve.bn_aggr(mv2[:, r, :], bn2[:, r, :]).then_inc(ln2_step, 1)
                st.wait(dve, ln2_step, S_OUT, 2, 2)
                st.wait(dve, rstd2_ready, S_OUT, 1, -1)
                dve.tensor_scalar(var2[:, r, :], mv2[:, r, 1:2], EPS, None, ALU.add).then_inc(var2_ready, 1)

            def quantise_x(st, part):
                r = st.ring(S_FFN)
                if part == 0:
                    st.wait(dve, rstd2_ready, S_FFN, 1, 1)
                    dve.tensor_scalar(xn2[:, r, :], x2[:, r, :], mv2[:, r, 0:1], rstd2[:, r, :],
                                      ALU.subtract, ALU.mult).then_inc(xq_step, 1)
                elif part == 1:
                    st.wait(dve, xq_step, S_FFN, 2, 1)
                    dve.tensor_scalar(xq_i[:, r, :], xn2[:, r, :], r_act[:, 0:1], None, ALU.mult).then_inc(xq_step, 1)
                else:
                    st.wait(dve, xq_step, S_FFN, 2, 2)
                    st.wait(dve, xqT_in_psum, S_FFN, 1, -1)
                    dve.tensor_scalar(xq[:, r, :], xq_i[:, r, :], QMIN, QMAX, ALU.max, ALU.min).then_inc(xq_ready, 1)

            def clip_h(st, half):
                r = st.ring(S_FFN)
                fs = slice(4 * half, 4 * half + 4)
                st.wait(dve, relu_done, S_FFN, 2, half + 1)
                st.wait(dve, y_in_psum, S_FFN, 1, -1)
                dve.tensor_scalar(hq[:, r, fs, :], h_i[:, r, fs, :], 0.0, HMAX, ALU.max, ALU.min).then_inc(hq_ready, 1)

            def output(st):
                r = st.ring(S_FFN)
                st.wait(dve, y_in_psum, S_FFN, 1, 1)
                st.wait(dve, x2_b_ready, S_FFN, 1, 1)
                st.wait_dma(dve, [stored, stored], S_FFN, 16, back=1)
                dve.scalar_tensor_tensor(out=y[:, r, :], in0=ps_misc[PIECE_BANK[YY]][:, 0:DIM], scalar=h_scale[:, 1:2],
                                         in1=x2_b[:, r, :], op0=ALU.mult, op1=ALU.add).then_inc(y_ready, 1)

            def while_filling(st, g):
                at = (st.s, g)
                if at == (0, 2):
                    rope_tables()
                elif at == (1, 3):
                    weight_maxima(0)
                elif at == (2, 0):
                    weight_maxima(1)
                elif at == (2, 2):
                    prepare_levels()
                elif at in ((2, 3), (2, 4)):
                    quantise_weights(g - 3)
                elif at == (4, 0):
                    prepare_scales()
                before = st.s * GROUPS + g - 1
                if before in WEIGHT_SLOTS:
                    copy_wT(dve, 2 * WEIGHT_SLOTS.index(before))
                if at == (4, 3):
                    round_b1()
                elif at == (4, 5):
                    round_b2()

            def body(st):
                for g in range(GROUPS):
                    norm_at = 0 if norm_early(st) else 4
                    if g == norm_at + 1 and st.has(S_NORM):
                        st.wait(dve, ln1_step, S_NORM, 2, 1)
                    if g == 7 and st.has(S_OUT):
                        st.wait(dve, ln2_step, S_OUT, 2, 1)
                    if st.has(S_MAX):
                        maxima(st, g)
                    if g == 0 and st.has(S_PROJ):
                        split_xT(st)
                    if g == 0 and st.has(S_FFN):
                        quantise_x(st, 0)
                    if g == 1 and st.has(S_FFN):
                        quantise_x(st, 1)
                    if g == norm_at and st.has(S_NORM):
                        norm1_stats(st)
                    if g == norm_at + 1 and st.has(S_NORM):
                        norm1_moments(st)
                    if g == 1 and st.has(S_ATT):
                        copy_maxima(st, 1, S_ATT)
                    if g == 1 and st.has(S_FFN):
                        quantise_x(st, 2)
                    if g == 1 and not st.looped and st.s == S_PROJ:
                        spread_tables()
                    if g == 5 and st.has(S_OUT):
                        split_attnT(st)
                    if g == norm_at + 1 and st.has(S_NORM):
                        norm1_variance(st)
                    if g == 1 and st.has(S_PROJ):
                        rope(st)
                    if g == norm_at + 2 and st.has(S_NORM):
                        norm1(st)
                    if g == 6 and st.has(S_OUT):
                        residual(st)
                    if g == 6 and st.has(S_FFN):
                        clip_h(st, 1)
                    if g == 6 and st.has(S_OUT):
                        norm2_stats(st)
                    if not st.looped:
                        while_filling(st, g)
                    if g == 3 and st.has(S_OUT):
                        normalise(st)
                    if g == 4 and st.has(S_MAX):
                        copy_maxima(st, 0, S_MAX)
                    if g == 5 and st.has(S_FFN):
                        clip_h(st, 0)
                    if g == 7 and st.has(S_OUT):
                        norm2_moments(st)
                    if g == 7 and st.has(S_FFN):
                        output(st)

            run_steps(dve, body)

        @block.tensor
        def _(pe):
            def mm(out, lhsT, rhs, start=True, stop=True, **kw):
                return pe.matmul(out, lhsT, rhs, start=start, stop=stop, skip_group_check=True, **kw)

            def transpose(out, in_, idn):
                return mm(out, in_, idn, is_transpose=True)

            emptied = {
                XT: (xT_lo_ready, S_PROJ, 1, 1), SQ0: (q_ready, S_STACK, 2, 1), MX1: (mxT_ready, S_ATT, 2, 2),
                QK: (rope_terms, S_PROJ, 3, 3), AT1: (attn_ready, S_OUT, 1, 1), XQ: (xqT_ready, S_FFN, 1, 1),
                SQ1: (q_ready, S_STACK, 2, 2), H0: (relu_done, S_FFN, 2, 1), AT2: (attnT_lo_ready, S_OUT, 1, 1),
                H1: (relu_done, S_FFN, 2, 2), WO: (x2_ready, S_OUT, 1, 1), MX0: (mxT_ready, S_MAX, 2, 1),
                VV: (v_copied, S_PROJ, 1, 1), SK0: (k_ready, S_STACK, 2, 1), YY: (y_ready, S_FFN, 1, 1),
                SK1: (k_ready, S_STACK, 2, 2),
            }

            def claim(st, piece):
                bank_n = PIECE_BANK[piece]
                for back in range(1, 2 * PIECES):
                    p = (piece - back) % PIECES
                    prev = Step(st.it, st.s + (piece - back) // PIECES, st.looped, st.held)
                    s_, stage, per, k = emptied[p]
                    if PIECE_BANK[p] == bank_n and prev.has(stage):
                        prev.wait(pe, s_, stage, per, k)
                        break
                return ps_misc[bank_n]

            def transpose_x(st):
                ps, r = claim(st, XT), st.ring(S_PROJ)
                st.wait(pe, xn_ready, S_PROJ, 1, 1)
                st.wait_dma(pe, c_loaded, S_PROJ, 16)
                for c in range(DC):
                    transpose(ps[:, 128 * c:128 * c + 128], xn[:, r, 128 * c:128 * c + 128], ident[:, :])
                transpose(ps[:, DIM:DIM + CTX], c_in[:, r, :], ident[:, :]).then_inc(xT_in_psum, 1)

            def split_product(st, out, terms, lo_ready_sem, stage):
                passes = [(x_hi, w) for x_hi, _, w_hi, w_lo in terms for w in (w_hi, w_lo)]
                passes += [(x_lo, w_hi) for _, x_lo, w_hi, _ in terms]
                for n, (x_part, w_part) in enumerate(passes):
                    if n == 2 * len(terms):
                        st.wait(pe, lo_ready_sem, stage, 1, 1)
                    ins = mm(out, x_part, w_part, n == 0, n == len(passes) - 1)
                return ins

            def x_terms(r, c, w_hi, w_lo):
                cols = slice(128 * c, 128 * c + 128)
                return xT_hi[:, r, cols], xT_lo[:, r, cols], w_hi, w_lo

            def project_qk(st):
                ps, r = claim(st, QK), st.ring(S_PROJ)
                if not st.looped and st.s == S_PROJ:
                    pe.wait_ge(w_lo_ready, 2)
                st.wait(pe, xT_hi_ready, S_PROJ, 1, 1)
                keys = [x_terms(r, DC, wkv_hi[:, 0:DIM], wkv_lo[:, 0:DIM])]
                queries = [x_terms(r, c, wq_hi[:, c, :], wq_lo[:, c, :]) for c in range(DC)]
                split_product(st, ps[:, 0:DIM], queries, xT_lo_ready, S_PROJ)
                split_product(st, ps[:, DIM:2 * DIM], keys, xT_lo_ready, S_PROJ).then_inc(qk_in_psum, 1)

            def project_v(st):
                ps, r = claim(st, VV), st.ring(S_PROJ)
                values = [x_terms(r, DC, wkv_hi[:, DIM:2 * DIM], wkv_lo[:, DIM:2 * DIM])]
                split_product(st, ps[:, 0:DIM], values, xT_lo_ready, S_PROJ).then_inc(v_in_psum, 1)

            def transpose_rows(st, piece, rows, in_psum, ready, half):
                ps, r = claim(st, piece), st.ring(S_STACK)
                st.wait(pe, lo_ready, S_STACK, 2, ready)
                for g in range(4):
                    h = 4 * (4 * half + g)
                    ins = transpose(ps[:, 128 * g:128 * g + 128], rows[:, r, h:h + 4, :].rearrange("p h c -> p (h c)"),
                                    ident[:, :])
                ins.then_inc(in_psum, 1)

            def scores_for_max(st, g):
                r = st.ring(S_MAX)
                if g % 4 == 0:
                    st.wait_dma(pe, diag_placed[g // 4], S_MAX, 64)
                    st.wait(pe, k_ready, S_MAX, 2, g // 4 + 1)
                st.wait(pe, max_done, S_MAX, GROUPS, g - 1)
                keys = k_stack[:, r, g, :].bitcast(BF16).rearrange("p (t w) -> p t w", w=2)[:, :, 1]
                queries = q_diag[:, r, g, :].bitcast(BF16).rearrange("p (t w) -> p t w", w=2)[:, :, 1]
                for i in range(4):
                    rows = slice(0, 96 if i < 3 else 128)
                    ins = mm(ps_max[g % 2][:, 128 * i:128 * i + 128], queries[rows, 128 * i:128 * i + 128], keys[rows])
                ins.then_inc(max_scores, 1)

            def transpose_maxima(st, half, stage, piece):
                ps, r = claim(st, piece), st.ring(stage)
                st.wait(pe, max_done, stage, GROUPS, 4 * half + 4)
                transpose(ps[0:16, 0:128], mx[:, r, 16 * half:16 * half + 16], ident[:, :]).then_inc(mx_in_psum, 1)

            def scores_for_exp(st, g):
                r = st.ring(S_ATT)
                if g % 4 == 0:
                    st.wait_dma(pe, neg_placed[g // 4], S_ATT, 16)
                st.wait(pe, exp_done, S_ATT, GROUPS, g - 1)
                mm(ps_exp[g % 2][:, :], k_stack[:, r, g, :], q_diag[:, r, g, :]).then_inc(exp_scores, 1)

            def weigh_values(st, g, stage):
                r = st.ring(stage)
                st.wait(pe, exp_done, stage, GROUPS, g + 1)
                if g == 0:
                    st.wait(pe, v_ready, stage, 1, 1)
                    st.wait(pe, av_copied, stage, 1, 0)
                region = g // VREG
                ps = ps_av[:, 128 * region:128 * region + 128]
                for i in range(4):
                    ins = mm(ps[32 * i:32 * i + 32, :], v_strip[:, r, 4 * g + i, :], expo[:, g % EXPO, 128 * i:128 * i + 128],
                             g % VREG == 0, g % VREG == VREG - 1 or g == GROUPS - 1)
                ins.then_inc(av_done, 1)

            def transpose_av(st):
                ps, r = claim(st, AT1), st.ring(S_OUT)
                st.wait(pe, av_copied, S_OUT, 1, 1)
                for c in range(3):
                    ins = transpose(ps[:, 128 * c:128 * c + 128], av[:, r, 128 * c:128 * c + 128], ident[:, :])
                ins.then_inc(attn_in_psum, 1)

            def transpose_attn(st):
                ps, r = claim(st, AT2), st.ring(S_OUT)
                st.wait(pe, attn_ready, S_OUT, 1, 1)
                for c in range(DC):
                    ins = transpose(ps[:, 128 * c:128 * c + 128], attn[:, r, 128 * c:128 * c + 128], ident[:, :])
                ins.then_inc(attnT_in_psum, 1)

            def project_out(st):
                ps, r = claim(st, WO), st.ring(S_OUT)
                if not st.looped and st.s == S_OUT:
                    pe.wait_ge(w_lo_ready, 3)
                st.wait(pe, attnT_hi_ready, S_OUT, 1, 1)
                terms = [(attnT_hi[:, r, 128 * c:128 * c + 128], attnT_lo[:, r, 128 * c:128 * c + 128],
                          wout_hi[:, c, :], wout_lo[:, c, :]) for c in range(DC)]
                split_product(st, ps[:, 0:DIM], terms, attnT_lo_ready, S_OUT).then_inc(wo_in_psum, 1)

            def transpose_xq(st):
                ps, r = claim(st, XQ), st.ring(S_FFN)
                st.wait(pe, xq_ready, S_FFN, 1, 1)
                for c in range(DC):
                    ins = transpose(ps[:, 64 * c:64 * c + 64].bitcast(BF16), xq[:, r, 128 * c:128 * c + 128],
                                    ident_bf[:, :])
                ins.then_inc(xqT_in_psum, 1)

            def hidden(st, half, piece):
                ps, r = claim(st, piece), st.ring(S_FFN)
                st.wait(pe, xqT_ready, S_FFN, 1, 1)
                for f in range(4):
                    for c in range(DC):
                        ins = mm(ps[:, 128 * f:128 * f + 128], w1T[:, c, 4 * half + f, :],
                                 xqT[:, r, 128 * c:128 * c + 128], c == 0, c == DC - 1)
                ins.then_inc(h_in_psum, 1)

            def project_y(st):
                ps, r = claim(st, YY), st.ring(S_FFN)
                for f in range(FC):
                    if f % 4 == 0:
                        st.wait(pe, hq_ready, S_FFN, 2, f // 4 + 1)
                    ins = mm(ps[:, 0:DIM], hq[:, r, f, :], w2T[:, f, :], f == 0, f == FC - 1)
                ins.then_inc(y_in_psum, 1)

            def transpose_weights(n):
                which, c, quarter = n // 4, n // 2 % 2, n % 2
                pe.wait_ge(wq_ready, which + 1)
                if n >= 2:
                    pe.wait_ge(wT_ready[n % 2], n // 2)
                ps = ps_exp[n % 2][:, 0:256].bitcast(BF16)
                for f in range(4):
                    fc = 4 * quarter + f
                    at = fc * DIM + 128 * c if which == 0 else c * FFN + 128 * fc
                    ins = transpose(ps[:, 128 * f:128 * f + 128], w_q[which][:, at:at + 128], ident_bf[:, :])
                ins.then_inc(wT_in_psum, 1)

            def body(st):
                if not st.looped and st.s == 0:
                    pe.wait_ge(id_ready, 2)
                    pe.wait_ge(ident_bf_ready, 1)
                    pe.wait_ge(early_loaded, EARLY)
                    pe.wait_ge(pads_ready, 3)
                for g in range(GROUPS):
                    if g < 2 and not st.looped and st.s == S_ATT:
                        pe.wait_ge(wT_ready[g], 4)
                    if st.has(S_MAX):
                        scores_for_max(st, g)
                    if g == 0 and st.has(S_PROJ):
                        transpose_x(st)
                    if g == 1 and st.has(S_ATT):
                        transpose_maxima(st, 1, S_ATT, MX1)
                    if g == 2 and st.has(S_STACK):
                        transpose_rows(st, SQ1, q_rows, q_in_psum, 1, 1)
                    if g == 3 and st.has(S_OUT):
                        transpose_av(st)
                    if g == 4 and st.has(S_STACK):
                        transpose_rows(st, SK0, k_rows, k_in_psum, 2, 0)
                    if g == 5 and st.has(S_OUT):
                        transpose_attn(st)
                    if g == 6 and st.has(S_OUT):
                        project_out(st)
                    if st.has(S_ATT):
                        scores_for_exp(st, g)
                    if g == 0 and st.has(S_STACK):
                        transpose_rows(st, SQ0, q_rows, q_in_psum, 1, 0)
                    if g == 1 and st.has(S_PROJ):
                        project_qk(st)
                    if g == 2 and st.has(S_FFN):
                        transpose_xq(st)
                    if g == 3 and st.has(S_FFN):
                        hidden(st, 0, H0)
                    if g == 4 and st.has(S_MAX):
                        transpose_maxima(st, 0, S_MAX, MX0)
                    if g == 5 and st.has(S_PROJ):
                        project_v(st)
                    if g == 5 and st.has(S_FFN):
                        hidden(st, 1, H1)
                    if g == 6 and st.has(S_STACK):
                        transpose_rows(st, SK1, k_rows, k_in_psum, 2, 1)
                    if g == 7 and st.has(S_FFN):
                        project_y(st)
                    at = st.s * GROUPS + g
                    if not st.looped and at in WEIGHT_SLOTS:
                        for n in range(2):
                            transpose_weights(2 * WEIGHT_SLOTS.index(at) + n)
                    if g < LAG and st.has(S_OUT):
                        weigh_values(st, GROUPS - LAG + g, S_OUT)
                    if g >= LAG and st.has(S_ATT):
                        weigh_values(st, g - LAG, S_ATT)

            run_steps(pe, body)


_INS = ['x', 'ctx_1024', 'fside_BxSx2_0', 'L0_xattn_Wq', 'L0_xattn_Wkv', 'L0_xattn_Wout', 'L0_xattn_bout',
        'L0_ffn_W1', 'L0_ffn_b1', 'L0_ffn_W2', 'L0_ffn_b2', 'L0_ffn_s_act1', 'L0_ffn_s_act2']


def kernel(**inputs):
    import numpy as _np
    import concourse.bacc as _bacc
    from concourse import mybir as _mybir
    from concourse.bass_utils import run_bass_kernel_spmd as _run

    nc = _bacc.Bacc("TRN2", target_bir_lowering=False, num_devices=1)
    arrays, args = {}, []
    for name in _INS:
        a = _np.ascontiguousarray(inputs[name])
        arrays[f"in_{name}_dram"] = a
        args.append(nc.dram_tensor(f"in_{name}_dram", a.shape, _mybir.dt.from_np(a.dtype), kind="ExternalInput").ap())
    args.append(nc.dram_tensor("out_dram", (BATCH, TOK, DIM), _mybir.dt.float32, kind="ExternalOutput").ap())
    xattn_ffn_kernel(nc, *args)
    r = _run(nc, [arrays], core_ids=[0])
    return r.results[0]["out_dram"]
```
